# Optimizing a Trainium2 kernel written in Bass

```python
import numpy as np
import jax
import jax.numpy as jnp

def _softmax(x, axis=-1):
    return jax.nn.softmax(x, axis=axis)

def _gelu(x):
    return jax.nn.gelu(x, approximate=True)

def _silu(x):
    return jax.nn.silu(x)

def _sigmoid(x):
    return jax.nn.sigmoid(x)

def _layernorm(x, axis=-1, eps=1e-05):
    m = jnp.mean(x, axis=axis, keepdims=True)
    v = jnp.var(x, axis=axis, keepdims=True)
    return (x - m) / jnp.sqrt(v + eps)

def _scatter_add(tgt, idx, src, axis=0):
    return tgt.at[idx].add(src)

def _segment_sum(src, seg, n):
    return jax.ops.segment_sum(src, seg, n)
kernel_name = 'mk_sandwich_d2_jaxref_r8_d9925b'

def setup_inputs(seed: int=0):
    np.random.seed(seed)
    _w = jnp.asarray

    def _L0_attn_setup():
        import jax, jax.numpy as jnp
        import numpy as np
        N_HEADS = 16
        HEAD_DIM = 64
        HIDDEN = 128
        key = jax.random.key(seed)
        kx, kq, kk, kv, ko = jax.random.split(key, 5)
        B, S = (1, 512)
        lim = float(np.sqrt(6.0 / (HIDDEN + N_HEADS * HEAD_DIM)))
        x = jax.random.normal(kx, (B, S, HIDDEN), dtype=jnp.float32)
        wq = jax.random.uniform(kq, (N_HEADS * HEAD_DIM, HIDDEN), jnp.float32, -lim, lim)
        wk = jax.random.uniform(kk, (N_HEADS * HEAD_DIM, HIDDEN), jnp.float32, -lim, lim)
        wv = jax.random.uniform(kv, (N_HEADS * HEAD_DIM, HIDDEN), jnp.float32, -lim, lim)
        wo = jax.random.uniform(ko, (HIDDEN, N_HEADS * HEAD_DIM), jnp.float32, -lim, lim)
        return {'x': x, 'wq': wq, 'wk': wk, 'wv': wv, 'wo': wo}
    _L0_attn_in = _L0_attn_setup()

    def _L0_ffn_setup():
        import math
        import jax, jax.numpy as jnp
        import numpy as np
        E = 8
        K = 2
        CF = 1.25
        D = 128
        F = 256
        B, S = (4, 256)
        key = jax.random.key(seed)
        ks = jax.random.split(key, 8)
        sd = 1.0 / math.sqrt(D)
        sf = 1.0 / math.sqrt(F)
        return {'x': jax.random.normal(ks[0], (B, S, D), jnp.float32), 'router_w': jax.random.normal(ks[1], (D, E), jnp.float32) * sd, 'router_b': jnp.zeros((E,), jnp.float32), 'w1': jax.random.normal(ks[2], (E, D, F), jnp.float32) * sd, 'b1': jax.random.normal(ks[3], (E, F), jnp.float32) * 0.01, 'w2': jax.random.normal(ks[4], (E, F, D), jnp.float32) * sf, 'b2': jax.random.normal(ks[5], (E, D), jnp.float32) * 0.01}
    _L0_ffn_in = _L0_ffn_setup()

    def _L1_attn_setup():
        import jax, jax.numpy as jnp
        import numpy as np
        import math
        D_MODEL = 128
        N_HEADS = 16
        DH = D_MODEL // N_HEADS
        THETA = 10000.0

        def _rope_tables(S):
            inv_freq = 1.0 / THETA ** (jnp.arange(0, DH, 2, dtype=jnp.float32) / DH)
            ang = jnp.arange(S, dtype=jnp.float32)[:, None] * inv_freq[None, :]
            cos = jnp.concatenate([jnp.cos(ang), jnp.cos(ang)], axis=-1)
            sin = jnp.concatenate([jnp.sin(ang), jnp.sin(ang)], axis=-1)
            return (cos, sin)

        def _apply_rope(x, cos, sin):
            x1, x2 = jnp.split(x, 2, axis=-1)
            rot = jnp.concatenate([-x2, x1], axis=-1)
            c = cos[None, :, None, :]
            s = sin[None, :, None, :]
            return x * c + rot * s
        key = jax.random.key(seed)
        k1, k2, k3 = jax.random.split(key, 3)
        x = jax.random.normal(k1, (4, 256, D_MODEL), dtype=jnp.float32)
        qkv = 0.01 * jax.random.normal(k2, (3 * D_MODEL, D_MODEL), dtype=jnp.float32)
        wo = 0.01 * jax.random.normal(k3, (D_MODEL, D_MODEL), dtype=jnp.float32)
        return {'x': x, 'qkv': qkv, 'wo': wo}
    _L1_attn_in = _L1_attn_setup()

    def _L1_ffn_setup():
        import jax, jax.numpy as jnp
        import numpy as np

        def _bitlinear(x, w_latent):
            scale = jax.lax.stop_gradient(jnp.clip(jnp.mean(jnp.abs(w_latent), axis=1, keepdims=True), 1e-05, None))
            tern = jnp.clip(jnp.round(w_latent / scale), -1.0, 1.0)
            w = w_latent + jax.lax.stop_gradient(tern - w_latent)
            return x @ (w * scale).T
        key = jax.random.key(seed)
        ks = jax.random.split(key, 6)
        dim, hidden, rank = (128, 512, 16)
        B, S = (4, 512)
        x = jax.random.normal(ks[0], (B, S, dim), dtype=jnp.float32)
        w_fc = 0.02 * jax.random.normal(ks[1], (hidden, dim), dtype=jnp.float32)
        w_proj = 0.02 * jax.random.normal(ks[2], (dim, hidden), dtype=jnp.float32)
        u = 0.02 * jax.random.normal(ks[3], (hidden, rank), dtype=jnp.float32)
        v = 0.02 * jax.random.normal(ks[4], (rank, dim), dtype=jnp.float32)
        fast_b = jax.random.normal(ks[5], (rank, rank), dtype=jnp.float32)
        gate = jnp.float32(0.05)
        return {'x': x, 'fast_b': fast_b, 'w_fc': w_fc, 'w_proj': w_proj, 'u': u, 'v': v, 'gate': gate}
    _L1_ffn_in = _L1_ffn_setup()
    _d = {'L0_attn_x': _L0_attn_in['x'], 'L0_attn_wq': _L0_attn_in['wq'], 'L0_attn_wk': _L0_attn_in['wk'], 'L0_attn_wv': _L0_attn_in['wv'], 'L0_attn_wo': _L0_attn_in['wo'], 'L0_ffn_router_w': _L0_ffn_in['router_w'], 'L0_ffn_router_b': _L0_ffn_in['router_b'], 'L0_ffn_w1': _L0_ffn_in['w1'], 'L0_ffn_b1': _L0_ffn_in['b1'], 'L0_ffn_w2': _L0_ffn_in['w2'], 'L0_ffn_b2': _L0_ffn_in['b2'], 'L1_attn_qkv': _L1_attn_in['qkv'], 'L1_attn_wo': _L1_attn_in['wo'], 'L1_ffn_fast_b': _L1_ffn_in['fast_b'], 'L1_ffn_w_fc': _L1_ffn_in['w_fc'], 'L1_ffn_w_proj': _L1_ffn_in['w_proj'], 'L1_ffn_u': _L1_ffn_in['u'], 'L1_ffn_v': _L1_ffn_in['v'], 'L1_ffn_gate': _L1_ffn_in['gate']}
    _x0 = _d['L0_attn_x']
    _d['L0_attn_x'] = jax.random.normal(jax.random.fold_in(jax.random.key(seed), 1), (2, 1024, 128), dtype=_x0.dtype)
    del _x0
    return _d

def reference(L0_attn_x, L0_attn_wq, L0_attn_wk, L0_attn_wv, L0_attn_wo, L0_ffn_router_w, L0_ffn_router_b, L0_ffn_w1, L0_ffn_b1, L0_ffn_w2, L0_ffn_b2, L1_attn_qkv, L1_attn_wo, L1_ffn_fast_b, L1_ffn_w_fc, L1_ffn_w_proj, L1_ffn_u, L1_ffn_v, L1_ffn_gate):

    def _L0_attn_ref(x, wq, wk, wv, wo):
        import jax, jax.numpy as jnp
        import numpy as np
        N_HEADS = 16
        HEAD_DIM = 64
        HIDDEN = 128
        B, S, _ = x.shape
        scale = HEAD_DIM ** (-0.5)

        def proj(w):
            return jnp.einsum('bsh,eh->bse', x, w).reshape(B, S, N_HEADS, HEAD_DIM).transpose(0, 2, 1, 3)
        q, k, v = (proj(wq), proj(wk), proj(wv))
        scores = jnp.einsum('bhqd,bhkd->bhqk', q, k) * scale
        causal = jnp.tril(jnp.ones((S, S), dtype=bool))
        scores = jnp.where(causal, scores, -jnp.inf)
        probs = jax.nn.softmax(scores, axis=-1)
        out = jnp.einsum('bhqk,bhkd->bhqd', probs, v)
        out = out.transpose(0, 2, 1, 3).reshape(B, S, N_HEADS * HEAD_DIM)
        return jnp.einsum('bse,he->bsh', out, wo)

    def _L0_ffn_ref(x, router_w, router_b, w1, b1, w2, b2):
        import math
        import jax, jax.numpy as jnp
        import numpy as np
        E = 8
        K = 2
        CF = 1.25
        D = 128
        F = 256
        B, S = (4, 256)
        b, s, d = x.shape
        xf = x.reshape(-1, d)
        T = b * s
        A = T * K
        cap = max(1, int(math.ceil(CF * A / E)))
        logits = xf @ router_w + router_b
        probs = jax.nn.softmax(logits, axis=-1)
        topk_p, topk_i = jax.lax.top_k(probs, K)
        topk_p = topk_p / jnp.clip(topk_p.sum(-1, keepdims=True), 1e-09)
        a_tok = jnp.repeat(jnp.arange(T), K)
        a_exp = topk_i.reshape(-1)
        a_w = topk_p.reshape(-1)
        order = jnp.argsort(a_exp)
        se, st, sw = (a_exp[order], a_tok[order], a_w[order])
        counts = jnp.bincount(se, length=E)
        starts = jnp.cumsum(counts) - counts
        rank = jnp.arange(A) - starts[se]
        keep = rank < cap
        slot = jnp.where(keep, se * cap + rank, E * cap)
        buf = jnp.zeros((E * cap + 1, d), x.dtype).at[slot].set(xf[st])
        buf = buf[:-1].reshape(E, cap, d)
        h = jax.nn.gelu(jnp.einsum('ecd,edf->ecf', buf, w1) + b1[:, None, :], approximate=False)
        eo = jnp.einsum('ecf,efd->ecd', h, w2) + b2[:, None, :]
        eo_flat = jnp.concatenate([eo.reshape(E * cap, d), jnp.zeros((1, d), x.dtype)], axis=0)
        w = jnp.where(keep, sw, 0.0)[:, None]
        out = jnp.zeros_like(xf).at[st].add(eo_flat[slot] * w)
        return out.reshape(b, s, d)

    def _L1_attn_ref(x, qkv, wo):
        import jax, jax.numpy as jnp
        import numpy as np
        import math
        D_MODEL = 128
        N_HEADS = 16
        DH = D_MODEL // N_HEADS
        THETA = 10000.0

        def _rope_tables(S):
            inv_freq = 1.0 / THETA ** (jnp.arange(0, DH, 2, dtype=jnp.float32) / DH)
            ang = jnp.arange(S, dtype=jnp.float32)[:, None] * inv_freq[None, :]
            cos = jnp.concatenate([jnp.cos(ang), jnp.cos(ang)], axis=-1)
            sin = jnp.concatenate([jnp.sin(ang), jnp.sin(ang)], axis=-1)
            return (cos, sin)

        def _apply_rope(x, cos, sin):
            x1, x2 = jnp.split(x, 2, axis=-1)
            rot = jnp.concatenate([-x2, x1], axis=-1)
            c = cos[None, :, None, :]
            s = sin[None, :, None, :]
            return x * c + rot * s
        B, S, D = x.shape
        QKV = x @ qkv.T
        Q, K, V = jnp.split(QKV, 3, axis=-1)
        q = Q.reshape(B, S, N_HEADS, DH)
        k = K.reshape(B, S, N_HEADS, DH)
        v = V.reshape(B, S, N_HEADS, DH)
        cos, sin = _rope_tables(S)
        q = _apply_rope(q, cos, sin)
        k = _apply_rope(k, cos, sin)
        q = q.transpose(0, 2, 1, 3)
        k = k.transpose(0, 2, 1, 3)
        v = v.transpose(0, 2, 1, 3)
        scores = jnp.einsum('bhsd,bhtd->bhst', q, k) / math.sqrt(float(DH))
        mask = jnp.tril(jnp.ones((S, S), dtype=scores.dtype))
        scores = scores * mask
        scores = jnp.where(scores == 0.0, -jnp.inf, scores)
        attn = jax.nn.softmax(scores, axis=-1)
        out = jnp.einsum('bhst,bhtd->bhsd', attn, v)
        out = out.transpose(0, 2, 1, 3).reshape(B, S, D)
        return out @ wo.T

    def _L1_ffn_ref(x, fast_b, w_fc, w_proj, u, v, gate):
        import jax, jax.numpy as jnp
        import numpy as np

        def _bitlinear(x, w_latent):
            scale = jax.lax.stop_gradient(jnp.clip(jnp.mean(jnp.abs(w_latent), axis=1, keepdims=True), 1e-05, None))
            tern = jnp.clip(jnp.round(w_latent / scale), -1.0, 1.0)
            w = w_latent + jax.lax.stop_gradient(tern - w_latent)
            return x @ (w * scale).T
        h = _bitlinear(x, w_fc) + gate * (x @ v.T @ fast_b.T @ u.T)
        r = jnp.maximum(h, 0.0)
        return _bitlinear(r * r, w_proj)
    x = L0_attn_x
    x = x + _layernorm(_L0_attn_ref(_layernorm(x, axis=-1), L0_attn_wq, L0_attn_wk, L0_attn_wv, L0_attn_wo), axis=-1)
    x = x + _layernorm(_L0_ffn_ref(_layernorm(x, axis=-1), L0_ffn_router_w, L0_ffn_router_b, L0_ffn_w1, L0_ffn_b1, L0_ffn_w2, L0_ffn_b2), axis=-1)
    x = x + _layernorm(_L1_attn_ref(_layernorm(x, axis=-1), L1_attn_qkv, L1_attn_wo), axis=-1)
    x = x + _layernorm(_L1_ffn_ref(_layernorm(x, axis=-1), L1_ffn_fast_b, L1_ffn_w_fc, L1_ffn_w_proj, L1_ffn_u, L1_ffn_v, L1_ffn_gate), axis=-1)
    return x

_drawn_inputs = setup_inputs


def setup_inputs(seed=0):
    import zlib

    import numpy as np

    out = dict(_drawn_inputs(seed))
    spreads = {'L0_ffn_router_b': (0.0, 0.1)}
    factors = {'L0_ffn_b1': 8.0,
     'L0_ffn_b2': 5.533,
     'L1_ffn_fast_b': 4.91,
     'L1_ffn_u': 4.953,
     'L1_ffn_v': 4.515}
    for name, (base, spread) in spreads.items():
        noise = np.random.default_rng([zlib.crc32(name.encode()), seed]).standard_normal(out[name].shape)
        drawn = base * np.exp(spread * noise) if base else spread * noise
        out[name] = jnp.asarray(drawn.astype(out[name].dtype))
    for name, factor in factors.items():
        out[name] = (out[name] * factor).astype(out[name].dtype)
    return out
```

```python
from contextlib import ExitStack

import numpy as np

import concourse.bass as bass
from concourse import mybir

F32 = mybir.dt.float32
BF16 = mybir.dt.bfloat16
U32 = mybir.dt.uint32
ALU = mybir.AluOpType
ACT = mybir.ActivationFunctionType
AX = mybir.AxisListType

P = 128
B, S, D = 2, 1024, 128
T = B * S
NT = T // P
ST = S // P
BANK = 512
TPB = BANK // P
NB = T // BANK
HEADS = 16
DH0 = 64
HPC = P // DH0
CH0 = HEADS // HPC
DH1 = D // HEADS
HPG = 4
G1 = HEADS // HPG
E, TOPK, F0 = 8, 2, 256
CAP = -(-T * TOPK * 5 // (E * 4))
FC0 = F0 // P
F1 = 512
FC1 = F1 // P
RANK = 16
NPROB = 3
EPS = 1e-5
MASKED = -1e30

C_IDENT, C_CAUSAL, C_UPPER, C_IOTA, C_HEADS, C_END = 0, 128, 256, 384, 392, 408


def constant_table():
    c = np.zeros((P, C_END), np.float32)
    i = np.arange(P)
    c[:, C_IDENT:C_IDENT + P] = np.eye(P)
    c[:, C_CAUSAL:C_CAUSAL + P] = np.where(i[None, :] > i[:, None], MASKED, 0.0)
    c[:, C_UPPER:C_UPPER + P] = i[:, None] < i[None, :]
    c[:, C_IOTA:C_IOTA + E] = np.arange(E)
    c[:, C_HEADS:C_HEADS + HEADS] = i[:, None] // DH1 == np.arange(HEADS)[None, :]
    return c


def rotary_table():
    inv = (1.0 / np.float32(10000.0) ** (np.arange(0, DH1, 2, dtype=np.float32) / np.float32(DH1))).astype(np.float32)
    angle = np.arange(S, dtype=np.float32)[None, :] * inv[:, None]
    cos, sin = np.cos(angle), np.sin(angle)
    cos8, sin8 = np.concatenate([cos, cos]), np.concatenate([-sin, sin])
    return np.ascontiguousarray(np.stack([np.tile(cos8, (HEADS, 1)), np.tile(sin8, (HEADS, 1))], 1), np.float32)


class Attention:

    def __init__(self, heads):
        self.heads = heads
        self.items = [(b, qt, h) for b in range(B) for qt in range(ST) for h in range(heads)]
        self.n = len(self.items)
        self.groups = B * ST
        self.rounds = []
        self.of_item = []
        copied = {"act": 0, "dve": 0}
        for i, (b, qt, h) in enumerate(self.items):
            mine = []
            for k0 in range(0, qt + 1, TPB):
                eng = "act" if len(self.rounds) % 2 == 0 else "dve"
                copied[eng] += 1
                mine.append(len(self.rounds))
                self.rounds.append((i, k0, min(TPB, qt + 1 - k0), eng, copied[eng]))
            self.of_item.append(mine)
        self.copied = copied

    def group(self, i):
        b, qt, h = self.items[i]
        return b * ST + qt

    def ends_group(self, i):
        return 0 <= i < self.n and self.items[i][2] == self.heads - 1


def build(nc, x, w0, wo0, router_w, router_b, w1, b1, w2, b2, wl1, wo1, fast_bT, w_fc, w_proj, uT, v, gate,
          consts, rotary, out):
    with ExitStack() as ctx:
        def sb(name, shape, dt=F32):
            return ctx.enter_context(nc.sbuf_tensor(name, shape, dt))

        def sem(name):
            return ctx.enter_context(nc.semaphore(name))

        X = sb("X", [P, NT, D])
        xn = sb("xn", [P, NT, D])
        xnT = sb("xnT", [P, T])
        stats = sb("stats", [P, NT, 6])
        mv = sb("mv", [P, NT, 2])
        rstd = sb("rstd", [P, NT])
        cst = sb("cst", [P, C_END])
        identb = sb("identb", [P, P], BF16)
        causalb = sb("causalb", [P, P], BF16)
        upperb = sb("upperb", [P, P], BF16)
        onesb = sb("onesb", [P, P], BF16)
        onesf = sb("onesf", [1, P])
        ident = cst[:, C_IDENT:C_IDENT + P]

        QT = sb("QT", [P, B, S])
        Kz = sb("Kz", [P, B, HPG, S])
        V = sb("V", [P, B, ST, P])
        probs = sb("probs", [P, NPROB, S])
        PT = sb("PT", [P, 2, HPG, S])
        den = sb("den", [P, 4, HPG])
        rden = sb("rden", [P, 2, HPG])
        rdb = sb("rdb", [P, 2, P])
        rs = sb("rs", [P, 2, P])
        nmax = sb("nmax", [P, 4])
        headm = sb("headm", [P, HPG])
        scratch = sb("scratch", [1, 1])
        credit = sb("credit", [1, 3])
        arena = sb("arena", [P, B * CH0 * S])
        attnT = arena[:, :].rearrange("p (b c s) -> p b c s", b=B, c=CH0)
        attn1T = arena[:, 0:B * G1 * S].rearrange("p (b g s) -> p b g s", b=B, g=G1)
        half = B * G1 * S
        Sm = arena[:, half:half + 2 * S].rearrange("p (i s) -> p i s", i=2)
        Zb = arena[:, half + 2 * S:half + 3 * S].bitcast(BF16).rearrange("p (i s) -> p i s", i=2)
        V1 = arena[:, half + 3 * S:half + 5 * S].rearrange("p (t e) -> p t e", t=NT)
        K1T = arena[:, half + 5 * S:half + 7 * S].rearrange("p (b s) -> p b s", b=B)
        hT = arena[:, 0:2 * FC0 * T].rearrange("p (i f t) -> p i f t", i=2, f=FC0)
        acc = arena[:, 2 * FC0 * T:2 * FC0 * T + T].rearrange("p (n d) -> p n d", n=NT)
        relu = arena[:, 0:FC1 * T].rearrange("p (f t) -> p f t", f=FC1)
        rot = PT[:, :, :, :].rearrange("p i h s -> p (i h) s")
        cs = probs[:, 0:2, :]

        w0s = sb("w0s", [P, 3, P])
        wo0s = sb("wo0s", [P, CH0, D])
        rws = sb("rws", [P, E])
        rbs = sb("rbs", [1, E])
        w1s = sb("w1s", [P, 2, F0])
        w2s = sb("w2s", [P, 2, FC0, D])
        b1s = sb("b1s", [P, E, FC0])
        b1e = sb("b1e", [P, 2, FC0])
        b2s = sb("b2s", [E, D])
        wl1s = sb("wl1s", [P, 5, P])
        wo1s = sb("wo1s", [P, G1, D])
        fbs = sb("fbs", [RANK, RANK])
        uTs = sb("uTs", [RANK, F1])
        vs = sb("vs", [RANK, D])
        gates = sb("gates", [RANK, 1])
        wfc = sb("wfc", [P, FC1, D])
        wpj = sb("wpj", [P, F1])
        wq_t = arena[:, half:half + 2 * F1].rearrange("p (i f) -> p i f", i=2)
        wsc = sb("wsc", [P, 8])
        lowA = arena[0:RANK, half + 4 * F1:half + 4 * F1 + D]
        w1e = arena[:, half + 2 * F1:half + 3 * F1]
        w2e = arena[:, half + 3 * F1:half + 4 * F1].rearrange("p (f d) -> p f d", f=FC1)

        spare = [Kz[:, b, 2, :] for b in range(B)]
        cut = NT * E

        def router(b, n, w=1):
            return spare[b][:, n * cut:(n + w) * cut].rearrange("p (n e) -> p n e", n=NT)

        lg, ex, top, before, wgt = (router(0, n) for n in range(5))
        idx = router(0, 5).bitcast(U32)
        sel = spare[1][:, 0:TOPK * cut].rearrange("p (k n e) -> p k n e", k=TOPK, n=NT)
        selb = spare[1][:, 2 * cut:2 * cut + cut // 2].bitcast(BF16).rearrange("p (n e) -> p n e", n=NT)
        beforeb = spare[1][:, 3 * cut:3 * cut + cut // 2].bitcast(BF16).rearrange("p (n e) -> p n e", n=NT)
        m1 = sb("m1", [P, NT])
        idxf = sb("idxf", [P, NT, TOPK])
        gsum = sb("gsum", [P, NT])
        wcol = sb("wcol", [P, 2, NT])
        wgT = arena[0:E, 2 * FC0 * T + T:2 * FC0 * T + 2 * T]

        pS = [ctx.enter_context(nc.psum_tensor(f"pS{i}", [P, 2 * BANK], F32)) for i in range(2)]
        pT = [ctx.enter_context(nc.psum_tensor(f"pT{i}", [P, BANK], F32)) for i in range(2)]
        pO = [ctx.enter_context(nc.psum_tensor(f"pO{i}", [P, BANK], F32)) for i in range(2)]
        bank = [pS[0][:, 0:BANK], pS[0][:, BANK:2 * BANK], pS[1][:, 0:BANK], pS[1][:, BANK:2 * BANK],
                pT[0][:, :], pT[1][:, :], pO[0][:, :], pO[1][:, :]]

        ld_x, ld_c = sem("ld_x"), sem("ld_c")
        ld_w0, ld_w = sem("ld_w0"), sem("ld_w")
        ld_rot = sem("ld_rot")
        ld_e = [sem("ld_e0"), sem("ld_e1")]
        const_ready = sem("const_ready")
        zeros_ready = sem("zeros_ready")
        st_ready = [sem(f"st_ready{k}") for k in range(8)]
        mv_ready = [sem(f"mv_ready{k}") for k in range(8)]
        var_ready = [sem(f"var_ready{k}") for k in range(8)]
        std_ready = [sem(f"std_ready{k}") for k in range(8)]
        rstd_ready = [sem(f"rstd_ready{k}") for k in range(8)]
        xn_ready = [sem(f"xn_ready{k}") for k in range(8)]
        x_added = [sem(f"x_added{k}") for k in range(4)]
        tr_done = [sem(f"tr_done{k}") for k in range(4)]
        xnT_ready = [sem(f"xnT_ready{k}") for k in range(4)]
        y_done = [sem(f"y_done{k}") for k in range(4)]
        names = ["proj", "ev_act", "ev_dve", "s", "mx", "z", "p", "t", "cp_act", "cp_dve", "rd1", "rd", "o", "rs", "n"]
        A = [{n: sem(f"a{k}_{n}") for n in names} for k in range(2)]
        headm_ready = sem("headm_ready")
        b1_ready = sem("b1_ready")
        kv_ready = [sem("kv_act"), sem("kv_dve")]
        rope = sem("rope")
        rope_in = sem("rope_in")
        rope_p = sem("rope_p")
        lg_done, lg_ready = sem("lg_done"), sem("lg_ready")
        r_ = sem("router_step")
        ex_ready = sem("ex_ready")
        rank_done = sem("rank_done")
        wgt_ready = sem("wgt_ready")
        wgT_done, wgT_ready = sem("wgT_done"), sem("wgT_ready")
        b2_done, acc_ready = sem("b2_done"), sem("acc_ready")
        wcol_ready = sem("wcol_ready")
        up_done, h_ready, down_done, added = sem("up_done"), sem("h_ready"), sem("down_done"), sem("added")
        q_ = sem("quant_step")
        lowA_done, lowA_ready = sem("lowA_done"), sem("lowA_ready")
        w1e_done, w1e_ready = sem("w1e_done"), sem("w1e_ready")
        w2e_done, w2e_ready = sem("w2e_done"), sem("w2e_ready")
        wT_ready = sem("wT_ready")
        fc_done, relu_ready, sq_ready = sem("fc_done"), sem("relu_ready"), sem("sq_ready")
        out_ready, stored = sem("out_ready"), sem("stored")

        L = [Attention(HPC), Attention(HPG)]
        block = ctx.enter_context(nc.Block())

        @block.sync
        def _(sp):
            for j in range(NB):
                sp.dma_start(X[:, j * TPB:(j + 1) * TPB, :],
                             x[j * BANK:(j + 1) * BANK, :].rearrange("(n p) d -> p n d", p=P)).then_inc(ld_x, 16)
            sp.dma_start(cst[:, :], consts).then_inc(ld_c, 16)
            sp.dma_start(w0s[:, :, :], w0[0, :, :, :]).then_inc(ld_w0, 16)
            for dst, src in ((wo0s[:, :, :], wo0.rearrange("(c p) d -> p c d", p=P)),
                             (rws[:, :], router_w), (rbs[:, :], router_b),
                             (b1s[:, :, :], b1), (b2s[:, :], b2),
                             (wl1s[:, :, :], wl1), (wo1s[:, :, :], wo1),
                             (fbs[:, :], fast_bT), (uTs[:, :], uT), (vs[:, :], v),
                             (gates[:, :], gate.to_broadcast([RANK, 1])),
                             (wfc[:, :, :], w_fc.rearrange("(c p) d -> p c d", p=P)), (wpj[:, :], w_proj)):
                sp.dma_start(dst, src).then_inc(ld_w, 16)
            for e in range(2):
                sp.dma_start(w1s[:, e, :], w1[e, :, :]).then_inc(ld_e[e], 16)
                sp.dma_start(w2s[:, e, :, :], w2[e, :, :].rearrange("(c p) d -> p c d", p=P)).then_inc(ld_e[e], 16)
            with sp.Fori(0, CH0 - 1) as c:
                sp.wait_ge(A[0]["proj"], c * 12 + 12)
                sp.dma_start(w0s[:, :, :], w0[bass.ds(c + 1, 1), :, :, :].rearrange("o p k e -> p (o k) e")).then_inc(ld_w0, 16)
            with sp.Fori(0, E // 2 - 1) as t:
                for e in range(2):
                    sp.wait_ge(down_done, (t * 2 + e) * NB + NB)
                    sp.dma_start(w1s[:, e, :], w1[bass.ds(t * 2 + 2 + e, 1), :, :].rearrange("o p f -> p (o f)")).then_inc(ld_e[e], 16)
                    sp.dma_start(w2s[:, e, :, :], w2[bass.ds(t * 2 + 2 + e, 1), :, :].rearrange("o (c p) d -> p (o c) d", p=P)).then_inc(ld_e[e], 16)
            sp.wait_ge(A[0]["o"], CH0 * L[0].groups)
            sp.dma_start(cs, rotary).then_inc(ld_rot, 16)
            for j in range(NB):
                sp.wait_ge(out_ready, j + 1)
                sp.dma_start(out[j * BANK:(j + 1) * BANK, :].rearrange("(n p) d -> p n d", p=P),
                             X[:, j * TPB:(j + 1) * TPB, :]).then_inc(stored, 16)
            sp.wait_ge(stored, 16 * NB)

        @block.gpsimd
        def _(pool):
            pool.memset(Kz[:, :, 0:HPC, :], 0.0).then_inc(zeros_ready, 1)
            pool.memset(onesb[:, :], 1.0).then_inc(zeros_ready, 1)
            pool.memset(onesf[:, :], 1.0).then_inc(zeros_ready, 1)
            for j, counted in enumerate((A[0]["n"], A[1]["n"], added)):
                pool.memset(credit[:, j:j + 1], 0.0).then_inc(counted, 1)
            for u in range(FC1 * NB):
                f, j = u % FC1, u // FC1
                r = relu[:, f, j * BANK:(j + 1) * BANK]
                pool.wait_ge(relu_ready, u + 1)
                pool.tensor_tensor(r, r, r, ALU.mult).then_inc(sq_ready, 1)

        @block.scalar
        def _(act):
            def std(k):
                act.wait_ge(var_ready[k], 1)
                nc.scalar.activation(rstd[:, :], rstd[:, :], ACT.Sqrt).then_inc(std_ready[k], 1)

            def copies_T(k):
                for j in range(0, NB, 2):
                    act.wait_ge(tr_done[k], j + 1)
                    nc.scalar.copy(xnT[:, j * BANK:(j + 1) * BANK], bank[j]).then_inc(xnT_ready[k], 1)

            def attention(k, it):
                a, plan = A[k], L[k]
                for i in range(plan.n + 2):
                    if 2 <= i:
                        for r in plan.of_item[i - 2]:
                            item, k0, nk, eng, count = plan.rounds[r]
                            if eng != "act":
                                continue
                            h, g = plan.items[item][2], plan.group(item)
                            act.wait_ge(a["t"], it * len(plan.rounds) + r + 1)
                            if g >= 2:
                                act.wait_ge(a["o"], it * plan.groups + g - 1)
                            nc.scalar.copy(PT[:, g % 2, h, k0 * P:(k0 + nk) * P], pT[r % 2][:, 0:nk * P])\
                                .then_inc(a["cp_act"], 1)
                    if i < plan.n:
                        b, qt, h = plan.items[i]
                        n, g = (qt + 1) * P, plan.group(i)
                        if i >= NPROB:
                            act.wait_ge(a["t"], it * len(plan.rounds) + plan.of_item[i - NPROB][-1] + 1)
                        if g >= 4 and h == 0:
                            act.wait_ge(a["rd1"], it * plan.groups + g - 3)
                        act.wait_ge(a["mx"], it * plan.n + i + 1)
                        if k == 0:
                            nc.scalar.activation(probs[:, i % NPROB, 0:n], pS[i % 2][:, 0:n], ACT.Exp,
                                                 bias=nmax[:, i % 4:i % 4 + 1],
                                                 accum_out=den[:, g % 4, h:h + 1]).then_inc(a["p"], 1)
                        else:
                            nc.scalar.activation(probs[:, i % NPROB, 0:n], Sm[:, i % 2, 0:n], ACT.Exp,
                                                 bias=nmax[:, i % 4:i % 4 + 1], scale=-1.0,
                                                 accum_out=den[:, g % 4, h:h + 1]).then_inc(a["p"], 1)

            std(0)
            copies_T(0)
            act.wait_ge(zeros_ready, 1)
            with act.Fori(0, CH0) as c:
                a = A[0]
                for u in range(0, 12, 2):
                    b, what, j = u // 6, (u % 6) // 2, u % 2
                    act.wait_ge(a["proj"], c * 12 + u + 1)
                    cols = slice(j * BANK, (j + 1) * BANK)
                    if what == 0:
                        nc.scalar.mul(QT[:, b, cols], bank[u % 8], DH0 ** -0.5).then_inc(a["ev_act"], 1)
                    elif what == 1:
                        nc.scalar.copy(Kz[0:DH0, b, 0, cols], bank[u % 8][0:DH0, :])
                        nc.scalar.copy(Kz[DH0:P, b, 1, cols], bank[u % 8][DH0:P, :]).then_inc(a["ev_act"], 1)
                    else:
                        nc.scalar.copy(V[:, b, j * TPB:(j + 1) * TPB, :], bank[u % 8]).then_inc(a["ev_act"], 1)
                attention(0, c)
            std(4)

            std(1)
            copies_T(1)
            act.wait_ge(r_, 2)
            nc.scalar.activation(ex[:, :, :], lg[:, :, :], ACT.Exp).then_inc(ex_ready, 1)
            with act.Fori(0, E // 2) as t:
                for e in range(2):
                    act.wait_ge(b1_ready, t * 2 + e + 1)
                    for u in range(FC0 * NB):
                        f, j = u % FC0, u // FC0
                        act.wait_ge(up_done, (t * 2 + e) * (FC0 * NB) + u + 1)
                        nc.scalar.activation(hT[:, e, f, j * BANK:(j + 1) * BANK], bank[u % 4], ACT.Gelu,
                                             bias=b1e[:, e, f:f + 1])\
                            .then_inc(h_ready, 1)
            std(5)

            std(2)
            copies_T(2)
            for u in range(16):
                act.wait_ge(A[1]["proj"], u + 1)
                nc.scalar.copy(rot[:, u // 2, (u % 2) * BANK:(u % 2 + 1) * BANK], bank[u % 8]).then_inc(rope_in, 1)
            for u in range(4):
                act.wait_ge(A[1]["proj"], 16 + u + 1)
                nc.scalar.copy(V1[:, u * TPB:(u + 1) * TPB, :], bank[u % 8]).then_inc(rope_in, 1)
            act.wait_ge(rope, 12)
            with act.Fori(0, G1) as g:
                act.wait_ge(headm_ready, g + 1)
                for b in range(B):
                    for h in range(0, HPG, 2):
                        nc.scalar.activation(Kz[:, b, h, :], K1T[:, b, :], ACT.Copy,
                                             scale=headm[:, h:h + 1]).then_inc(kv_ready[0], 1)
                attention(1, g)
            std(6)

            std(3)
            copies_T(3)
            for u in range(FC1 * NB):
                f, j = u % FC1, u // FC1
                act.wait_ge(fc_done, u + 1)
                nc.scalar.activation(relu[:, f, j * BANK:(j + 1) * BANK], bank[4 + u % 4], ACT.Relu).then_inc(relu_ready, 1)
            std(7)

        @block.vector
        def _(dve):
            def moments(k, tile, ready):
                for n in range(NT):
                    ready(n)
                    i = nc.vector.bn_stats(stats[:, n, :], tile(n))
                i.then_inc(st_ready[k], 1)
                dve.wait_ge(st_ready[k], 1)
                for n in range(NT):
                    i = nc.vector.bn_aggr(mv[:, n, :], stats[:, n, :])
                i.then_inc(mv_ready[k], 1)
                dve.wait_ge(mv_ready[k], 1)
                nc.vector.tensor_scalar_add(rstd[:, :], mv[:, :, 1], EPS).then_inc(var_ready[k], 1)
                dve.wait_ge(std_ready[k], 1)
                nc.vector.reciprocal(rstd[:, :], rstd[:, :]).then_inc(rstd_ready[k], 1)
                dve.wait_ge(rstd_ready[k], 1)

            def norm(k, tile):
                for n in range(NT):
                    nc.vector.tensor_scalar(xn[:, n, :], tile(n), mv[:, n, 0:1], rstd[:, n:n + 1],
                                            ALU.subtract, ALU.mult).then_inc(xn_ready[k], 1)

            def before_block(k, ready):
                moments(k, lambda n: X[:, n, :], ready)
                norm(k, lambda n: X[:, n, :])
                for j in range(1, NB, 2):
                    dve.wait_ge(tr_done[k], j + 1)
                    nc.vector.tensor_copy(xnT[:, j * BANK:(j + 1) * BANK], bank[j]).then_inc(xnT_ready[k], 1)

            def after_block(k, tile, ready):
                moments(4 + k, tile, ready)
                norm(4 + k, tile)
                for j in range(NB):
                    dve.wait_ge(xn_ready[4 + k], (j + 1) * TPB)
                    t = slice(j * TPB, (j + 1) * TPB)
                    i = nc.vector.tensor_tensor(X[:, t, :], X[:, t, :], xn[:, t, :], ALU.add)
                    i.then_inc(x_added[k], 1)
                    if k == 3:
                        pass

            def y_tile(n):
                return bank[n // TPB][:, (n % TPB) * P:(n % TPB + 1) * P]

            def attention(k, it, put):
                a, plan = A[k], L[k]
                nr = len(plan.rounds)
                for i in range(plan.n + 4):
                    if i < plan.n:
                        b, qt, h = plan.items[i]
                        n, g = (qt + 1) * P, plan.group(i)
                        dve.wait_ge(a["s"], it * plan.n + i + 1)
                        if k == 0:
                            if i >= 4:
                                dve.wait_ge(a["p"], it * plan.n + i - 3)
                            nc.vector.tensor_reduce(nmax[:, i % 4:i % 4 + 1], pS[i % 2][:, 0:n], AX.X, ALU.max,
                                                    negate=True).then_inc(a["mx"], 1)
                        else:
                            if i >= 2:
                                dve.wait_ge(a["p"], it * plan.n + i - 1)
                            nc.vector.tensor_scalar(Zb[:, i % 2, 0:n], pS[i % 2][:, 0:n], 0.0, MASKED,
                                                    ALU.is_equal, ALU.mult).then_inc(a["z"], 1)
                            dve.wait_ge(a["z"], it * plan.n + i + 1)
                            nc.vector.memset(scratch[:, :], 0.0)
                            nc.vector.tensor_tensor_reduce(Sm[:, i % 2, 0:n], pS[i % 2][:, 0:n], Zb[:, i % 2, 0:n],
                                                           -(DH1 ** -0.5), 3e38, ALU.add, ALU.min,
                                                           nmax[:, i % 4:i % 4 + 1]).then_inc(a["mx"], 1)
                    if 2 <= i < plan.n + 2:
                        for r in plan.of_item[i - 2]:
                            item, k0, nk, eng, count = plan.rounds[r]
                            if eng != "dve":
                                continue
                            hh, gg = plan.items[item][2], plan.group(item)
                            dve.wait_ge(a["t"], it * nr + r + 1)
                            if gg >= 2:
                                dve.wait_ge(a["o"], it * plan.groups + gg - 1)
                            nc.vector.tensor_copy(PT[:, gg % 2, hh, k0 * P:(k0 + nk) * P], pT[r % 2][:, 0:nk * P])\
                                .then_inc(a["cp_dve"], 1)
                    if plan.ends_group(i - 2):
                        gg = plan.group(i - 2)
                        dve.wait_ge(a["p"], it * plan.n + i - 1)
                        nc.vector.reciprocal(rden[:, gg % 2, 0:plan.heads], den[:, gg % 4, 0:plan.heads]).then_inc(a["rd1"], 1)
                        dve.wait_ge(a["rd1"], it * plan.groups + gg + 1)
                        if gg >= 2:
                            dve.wait_ge(a["o"], it * plan.groups + gg - 1)
                        nc.vector.tensor_copy(
                            rdb[:, gg % 2, :].rearrange("p (h w) -> p h w", h=plan.heads),
                            rden[:, gg % 2, 0:plan.heads].rearrange("p (h o) -> p h o", o=1).to_broadcast([P, plan.heads, P // plan.heads]))\
                            .then_inc(a["rd"], 1)
                    if plan.ends_group(i - 4):
                        gg = plan.group(i - 4)
                        dve.wait_ge(a["o"], it * plan.groups + gg + 1)
                        nc.vector.tensor_copy(rs[:, gg % 2, :], pO[gg % 2][:, P:2 * P]).then_inc(a["rs"], 1)
                        dve.wait_ge(a["rs"], it * plan.groups + gg + 1)
                        nc.vector.tensor_tensor(put(gg // ST, gg % ST), pO[gg % 2][:, 0:P], rs[:, gg % 2, :],
                                                ALU.mult).then_inc(a["n"], 1)

            dve.wait_ge(ld_c, 16)
            nc.vector.tensor_copy(identb[:, :], ident)
            nc.vector.tensor_copy(causalb[:, :], cst[:, C_CAUSAL:C_CAUSAL + P])
            nc.vector.tensor_copy(upperb[:, :], cst[:, C_UPPER:C_UPPER + P]).then_inc(const_ready, 1)

            before_block(0, lambda n: dve.wait_ge(ld_x, 16 * (n // TPB + 1)))
            dve.wait_ge(zeros_ready, 1)
            with dve.Fori(0, CH0) as c:
                a = A[0]
                for u in range(1, 12, 2):
                    b, what, j = u // 6, (u % 6) // 2, u % 2
                    dve.wait_ge(a["proj"], c * 12 + u + 1)
                    cols = slice(j * BANK, (j + 1) * BANK)
                    if what == 0:
                        nc.vector.tensor_scalar_mul(QT[:, b, cols], bank[u % 8], DH0 ** -0.5).then_inc(a["ev_dve"], 1)
                    elif what == 1:
                        nc.vector.tensor_copy(Kz[0:DH0, b, 0, cols], bank[u % 8][0:DH0, :])
                        nc.vector.tensor_copy(Kz[DH0:P, b, 1, cols], bank[u % 8][DH0:P, :]).then_inc(a["ev_dve"], 1)
                    else:
                        nc.vector.tensor_copy(V[:, b, j * TPB:(j + 1) * TPB, :], bank[u % 8]).then_inc(a["ev_dve"], 1)
                attention(0, c, lambda b, qt: attnT[:, b, bass.ds(c, 1), qt * P:(qt + 1) * P].rearrange("p o q -> p (o q)"))

            def y_ready(k):
                return lambda n: dve.wait_ge(y_done[k], n // TPB + 1)

            after_block(0, y_tile, y_ready(0))
            before_block(1, lambda n: dve.wait_ge(x_added[0], n // TPB + 1))

            dve.wait_ge(lg_done, 1)
            logits = bank[4][:, 0:NT * E].rearrange("p (n e) -> p n e", n=NT)
            nc.vector.tensor_reduce(m1[:, :], logits, AX.X, ALU.max).then_inc(r_, 1)
            dve.wait_ge(r_, 1)
            nc.vector.tensor_tensor(lg[:, :, :], logits,
                                    m1[:, :].rearrange("p (n o) -> p n o", o=1).to_broadcast([P, NT, E]),
                                    ALU.subtract).then_inc(r_, 1)
            dve.wait_ge(ex_ready, 1)
            for n in range(NT):
                i = nc.vector.max(top[:, n, :], ex[:, n, :])
            i.then_inc(r_, 1)
            dve.wait_ge(r_, 3)
            for n in range(NT):
                i = nc.vector.max_index(idx[:, n, :], top[:, n, :], ex[:, n, :])
            i.then_inc(r_, 1)
            dve.wait_ge(r_, 4)
            nc.vector.tensor_copy(idxf[:, :, :], idx[:, :, 0:TOPK]).then_inc(r_, 1)
            dve.wait_ge(r_, 5)
            experts = cst[:, C_IOTA:C_IOTA + E].rearrange("p (o e) -> p o e", o=1).to_broadcast([P, NT, E])
            for k in range(TOPK):
                i = nc.vector.tensor_tensor(sel[:, k, :, :], experts, idxf[:, :, k:k + 1].to_broadcast([P, NT, E]),
                                            ALU.is_equal)
            i.then_inc(r_, 1)
            dve.wait_ge(r_, 6)
            nc.vector.tensor_tensor(sel[:, 0, :, :], sel[:, 0, :, :], sel[:, 1, :, :], ALU.add).then_inc(r_, 1)
            dve.wait_ge(r_, 7)
            nc.vector.tensor_copy(selb[:, :, :], sel[:, 0, :, :])
            nc.vector.tensor_tensor(wgt[:, :, :], sel[:, 0, :, :], ex[:, :, :], ALU.mult)
            nc.vector.memset(before[:, 0, :], 0.0).then_inc(r_, 1)
            for n in range(1, NT):
                dve.wait_ge(r_, 7 + n)
                nc.vector.tensor_tensor(before[:, n, :], before[:, n - 1, :], sel[:, 0, n - 1, :], ALU.add).then_inc(r_, 1)
            dve.wait_ge(r_, 7 + NT)
            nc.vector.tensor_copy(beforeb[:, :, :], before[:, :, :]).then_inc(r_, 1)
            nc.vector.tensor_reduce(gsum[:, :], wgt[:, :, :], AX.X, ALU.add).then_inc(r_, 1)
            dve.wait_ge(r_, 9 + NT)
            nc.vector.reciprocal(gsum[:, :], gsum[:, :]).then_inc(r_, 1)
            dve.wait_ge(r_, 10 + NT)
            nc.vector.tensor_tensor(wgt[:, :, :], wgt[:, :, :],
                                    gsum[:, :].rearrange("p (n o) -> p n o", o=1).to_broadcast([P, NT, E]), ALU.mult).then_inc(r_, 1)
            dve.wait_ge(rank_done, 1)
            nc.vector.tensor_scalar(sel[:, 1, :, :], bank[5][:, 0:NT * E].rearrange("p (n e) -> p n e", n=NT),
                                    float(CAP), None, ALU.is_lt).then_inc(r_, 1)
            dve.wait_ge(r_, 12 + NT)
            nc.vector.tensor_tensor(wgt[:, :, :], wgt[:, :, :], sel[:, 1, :, :], ALU.mult).then_inc(wgt_ready, 1)
            for j in range(NB):
                dve.wait_ge(wgT_done, j + 1)
                nc.vector.tensor_copy(wgT[:, j * BANK:(j + 1) * BANK], bank[j][0:E, :]).then_inc(wgT_ready, 1)
            for j in range(NB):
                dve.wait_ge(b2_done, j + 1)
                nc.vector.tensor_copy(acc[:, j * TPB:(j + 1) * TPB, :], bank[4 + j]).then_inc(acc_ready, 1)
            with dve.Fori(0, E // 2) as t:
                for e in range(2):
                    nc.vector.tensor_copy(b1e[:, e, :], b1s[:, bass.ds(t * 2 + e, 1), :].rearrange("p o f -> p (o f)"))\
                        .then_inc(b1_ready, 1)
                    nc.vector.tensor_copy(wcol[:, e, :], wgt[:, :, bass.ds(t * 2 + e, 1)].rearrange("p n o -> p (n o)"))\
                        .then_inc(wcol_ready, 1)
                    dve.wait_ge(wcol_ready, t * 2 + e + 1)
                    if e == 0:
                        dve.wait_ge(acc_ready, NB)
                    for n in range(NT):
                        if n % TPB == 0:
                            dve.wait_ge(down_done, (t * 2 + e) * NB + n // TPB + 1)
                        dve.wait_ge(added, (t * 2 + e) * NT + n + 1)
                        nc.vector.scalar_tensor_tensor(acc[:, n, :], bank[4 + n // TPB][:, (n % TPB) * P:(n % TPB + 1) * P],
                                                       wcol[:, e, n:n + 1], acc[:, n, :], ALU.mult, ALU.add).then_inc(added, 1)
            after_block(1, lambda n: acc[:, n, :], lambda n: dve.wait_ge(added, E * NT + 1))

            before_block(2, lambda n: dve.wait_ge(x_added[1], n // TPB + 1))
            dve.wait_ge(ld_rot, 16)
            for b in range(B):
                for w in range(2):
                    s0 = 4 * b + 2 * w
                    dve.wait_ge(rope_in, 2 * (s0 + 2))
                    dst = QT[:, b, :] if w == 0 else K1T[:, b, :]
                    nc.vector.tensor_tensor(rot[:, s0, :], rot[:, s0, :], cs[:, 0, :], ALU.mult).then_inc(rope, 1)
                    nc.vector.tensor_tensor(rot[:, s0 + 1, :], rot[:, s0 + 1, :], cs[:, 1, :], ALU.mult).then_inc(rope, 1)
                    dve.wait_ge(rope, 3 * (2 * b + w) + 2)
                    nc.vector.tensor_tensor(dst, rot[:, s0, :], rot[:, s0 + 1, :], ALU.add).then_inc(rope, 1)
            dve.wait_ge(rope, 12)
            dve.wait_ge(rope_in, 20)
            nc.vector.memset(V[:, :, :, :], 0.0).then_inc(kv_ready[1], 1)
            dve.wait_ge(kv_ready[1], 1)
            with dve.Fori(0, G1) as g:
                dve.wait_ge(A[1]["n"], g * L[1].groups + 1)
                nc.vector.memset(scratch[:, :], 0.0)
                nc.vector.tensor_copy(headm[:, :], cst[:, bass.ds(g * HPG + C_HEADS, HPG)]).then_inc(headm_ready, 1)
                dve.wait_ge(headm_ready, g + 1)
                for b in range(B):
                    for h in range(1, HPG, 2):
                        nc.vector.tensor_scalar_mul(Kz[:, b, h, :], K1T[:, b, :], headm[:, h:h + 1])\
                            .then_inc(kv_ready[1], 1)
                nc.vector.tensor_copy(
                    V[:, :, :, :].rearrange("p b t (h w) -> p (b t) h w", h=HPG)[:, :, :, 0:DH1],
                    V1[:, :, bass.ds(g * (HPG * DH1), HPG * DH1)].rearrange("p t (h w) -> p t h w", h=HPG)).then_inc(kv_ready[1], 1)
                attention(1, g, lambda b, qt: attn1T[:, b, bass.ds(g, 1), qt * P:(qt + 1) * P].rearrange("p o q -> p (o q)"))
            after_block(2, y_tile, y_ready(2))

            dve.wait_ge(ld_w, 16 * 13)
            step = [0]

            def link(i):
                step[0] += 1
                i.then_inc(q_, 1)
                dve.wait_ge(q_, step[0])

            q0, q1 = wq_t[:, 0, :], wq_t[:, 1, :]

            def ternary(w, scale, t0, t1):
                link(nc.vector.tensor_scalar(wsc[:, 7:8], scale, 0.5, None, ALU.mult))
                link(nc.vector.tensor_scalar(t0, w, wsc[:, 7:8], None, ALU.is_gt))
                link(nc.vector.tensor_scalar(wsc[:, 6:7], scale, -0.5, None, ALU.mult))
                link(nc.vector.tensor_scalar(t1, w, wsc[:, 6:7], None, ALU.is_lt))
                link(nc.vector.tensor_tensor(t0, t0, t1, ALU.subtract))
                link(nc.vector.tensor_tensor(t0, t0, w, ALU.subtract))
                link(nc.vector.tensor_tensor(t0, t0, w, ALU.add))
                link(nc.vector.tensor_scalar(w, t0, scale, None, ALU.mult))

            link(nc.vector.tensor_reduce(wsc[:, 0:FC1], wfc[:, :, :], AX.X, ALU.add, apply_absolute_value=True))
            link(nc.vector.tensor_reduce(wsc[:, FC1:FC1 + 1], wpj[:, :], AX.X, ALU.add, apply_absolute_value=True))
            link(nc.vector.tensor_scalar(wsc[:, 0:FC1], wsc[:, 0:FC1], 1.0 / D, 1e-5, ALU.mult, ALU.max))
            link(nc.vector.tensor_scalar(wsc[:, FC1:FC1 + 1], wsc[:, FC1:FC1 + 1], 1.0 / F1, 1e-5, ALU.mult, ALU.max))
            for f in range(FC1):
                ternary(wfc[:, f, :], wsc[:, f:f + 1], q0[:, 0:D], q1[:, 0:D])
            ternary(wpj[:, :], wsc[:, FC1:FC1 + 1], q0, q1)
            nc.vector.memset(scratch[:, :], 0.0).then_inc(wT_ready, 1)
            dve.wait_ge(lowA_done, 1)
            nc.vector.tensor_scalar_mul(lowA[:, :], bank[4][0:RANK, 0:D], gates[:, 0:1]).then_inc(lowA_ready, 1)
            dve.wait_ge(w1e_done, 1)
            nc.vector.tensor_copy(q0, bank[6]).then_inc(q_, 1)
            dve.wait_ge(q_, step[0] + 1)
            nc.vector.tensor_tensor(w1e[:, :], bank[5], q0, ALU.add).then_inc(w1e_ready, 1)
            dve.wait_ge(w2e_done, 1)
            nc.vector.tensor_copy(w2e[:, :, :], bank[7]).then_inc(w2e_ready, 1)
            before_block(3, lambda n: dve.wait_ge(x_added[2], n // TPB + 1))
            moments(7, y_tile, y_ready(3))
            norm(7, y_tile)
            for j in range(NB):
                dve.wait_ge(xn_ready[7], (j + 1) * TPB)
                t = slice(j * TPB, (j + 1) * TPB)
                nc.vector.tensor_tensor(X[:, t, :], X[:, t, :], xn[:, t, :], ALU.add).then_inc(out_ready, 1)

        @block.tensor
        def _(pe):
            def transposes(k):
                for n in range(NT):
                    pe.wait_ge(xn_ready[k], n + 1)
                    i = nc.tensor.transpose(bank[n // TPB][:, (n % TPB) * P:(n % TPB + 1) * P], xn[:, n, :], ident)
                    if n % TPB == TPB - 1:
                        i.then_inc(tr_done[k], 1)
                pe.wait_ge(xnT_ready[k], NB)

            def attention(k, it):
                a, plan = A[k], L[k]
                nr = len(plan.rounds)
                w = P // plan.heads
                for i in range(plan.n + 3):
                    if i < plan.n:
                        b, qt, h = plan.items[i]
                        if i >= 2:
                            pe.wait_ge(a["p"] if k == 0 else a["mx"], it * plan.n + i - 1)
                        for c0 in range(0, qt + 1, TPB):
                            nk = min(TPB, qt + 1 - c0)
                            last = c0 + nk == qt + 1
                            m = nc.tensor.matmul(pS[i % 2][:, c0 * P:(c0 + nk) * P], QT[:, b, qt * P:(qt + 1) * P],
                                                 Kz[:, b, h, c0 * P:(c0 + nk) * P], start=True, stop=not last)
                        nc.tensor.matmul(pS[i % 2][:, qt * P:(qt + 1) * P], identb[:, :], causalb[:, :],
                                         start=False, stop=True).then_inc(a["s"], 1)
                    if 2 <= i < plan.n + 2:
                        pe.wait_ge(a["p"], it * plan.n + i - 1)
                        for r in plan.of_item[i - 2]:
                            item, k0, nk, eng, count = plan.rounds[r]
                            if r >= 2:
                                _, _, _, e2, c2 = plan.rounds[r - 2]
                                pe.wait_ge(a["cp_" + e2], it * plan.copied[e2] + c2)
                            for kt in range(nk):
                                m = nc.tensor.transpose(pT[r % 2][:, kt * P:(kt + 1) * P],
                                                        probs[:, item % NPROB, (k0 + kt) * P:(k0 + kt + 1) * P], ident)
                            m.then_inc(a["t"], 1)
                    if plan.ends_group(i - 3):
                        g = plan.group(i - 3)
                        b, qt = g // ST, g % ST
                        if g >= 2:
                            pe.wait_ge(a["n"], it * plan.groups + g)
                        pe.wait_ge(a["rd"], it * plan.groups + g + 1)
                        nc.tensor.matmul(pO[g % 2][:, P:2 * P], rdb[:, g % 2, :], ident, start=True, stop=True)
                        for e2 in ("act", "dve"):
                            done = max([plan.rounds[r][4] for j in range(i - 2) for r in plan.of_item[j]
                                        if plan.rounds[r][3] == e2], default=0)
                            if done:
                                pe.wait_ge(a["cp_" + e2], it * plan.copied[e2] + done)
                        for kt in range(qt + 1):
                            for h in range(plan.heads):
                                m = nc.tensor.matmul(pO[g % 2][h * w:(h + 1) * w, 0:P], V[:, b, kt, h * w:(h + 1) * w],
                                                     PT[:, g % 2, h, kt * P:(kt + 1) * P], start=(kt == 0), stop=(kt == qt),
                                                     skip_group_check=True)
                        m.then_inc(a["o"], 1)

            pe.wait_ge(const_ready, 1)
            transposes(0)
            with pe.Fori(0, CH0) as c:
                a = A[0]
                pe.wait_ge(a["n"], c * L[0].groups + 1)
                pe.wait_ge(ld_w0, c * 16 + 16)
                for u in range(12):
                    b, what, j = u // 6, (u % 6) // 2, u % 2
                    if u >= 8:
                        e2 = "ev_act" if u % 2 == 0 else "ev_dve"
                        pe.wait_ge(a[e2], c * 6 + (u - 8) // 2 + 1)
                    if what < 2:
                        m = nc.tensor.matmul(bank[u % 8], w0s[:, what, :], xnT[:, b * S + j * BANK:b * S + (j + 1) * BANK],
                                             start=True, stop=True)
                    else:
                        for t in range(TPB):
                            col = b * S + j * BANK + t * P
                            m = nc.tensor.matmul(bank[u % 8][:, t * P:(t + 1) * P], xnT[:, col:col + P], w0s[:, 2, :],
                                                 start=True, stop=True)
                    m.then_inc(a["proj"], 1)
                pe.wait_ge(a["ev_act"], c * 6 + 6)
                pe.wait_ge(a["ev_dve"], c * 6 + 6)
                attention(0, c)
            pe.wait_ge(A[0]["n"], CH0 * L[0].groups + 1)
            pe.wait_ge(ld_w, 16 * 13)
            for n in range(NT):
                for c in range(CH0):
                    m = nc.tensor.matmul(bank[n // TPB][:, (n % TPB) * P:(n % TPB + 1) * P],
                                         attnT[:, n // ST, c, (n % ST) * P:(n % ST + 1) * P], wo0s[:, c, :],
                                         start=(c == 0), stop=(c == CH0 - 1))
                if n % TPB == TPB - 1:
                    m.then_inc(y_done[0], 1)

            transposes(1)
            pe.wait_ge(zeros_ready, 3)
            for n in range(NT):
                o = bank[4][:, n * E:(n + 1) * E]
                nc.tensor.matmul(o, xnT[:, n * P:(n + 1) * P], rws[:, :], start=True, stop=False, skip_group_check=True)
                m = nc.tensor.matmul(o, onesf[:, :], rbs[:, :], start=False, stop=True, skip_group_check=True)
            m.then_inc(lg_done, 1)
            pe.wait_ge(r_, 8 + NT)
            nc.tensor.matmul(bank[5][:, 0:NT * E], upperb[:, :], selb[:, :, :], start=True, stop=False)
            nc.tensor.matmul(bank[5][:, 0:NT * E], onesb[:, :], beforeb[:, :, :], start=False, stop=True).then_inc(rank_done, 1)
            pe.wait_ge(wgt_ready, 1)
            for n in range(NT):
                m = nc.tensor.transpose(bank[n // TPB][0:E, (n % TPB) * P:(n % TPB + 1) * P], wgt[:, n, :], ident)
                if n % TPB == TPB - 1:
                    m.then_inc(wgT_done, 1)
            for n in range(NT):
                if n % TPB == 0:
                    pe.wait_ge(wgT_ready, n // TPB + 1)
                m = nc.tensor.matmul(bank[4 + n // TPB][:, (n % TPB) * P:(n % TPB + 1) * P], wgT[:, n * P:(n + 1) * P],
                                     b2s[:, :], start=True, stop=True)
                if n % TPB == TPB - 1:
                    m.then_inc(b2_done, 1)
            pe.wait_ge(acc_ready, NB)
            with pe.Fori(0, E // 2) as t:
                for e in range(2):
                    pe.wait_ge(ld_e[e], t * 32 + 32)
                    nu = FC0 * NB
                    for u in range(nu):
                        f, j = u % FC0, u // FC0
                        if u >= 4:
                            pe.wait_ge(h_ready, (t * 2 + e) * nu + u - 3)
                        m = nc.tensor.matmul(bank[u % 4], w1s[:, e, f * P:(f + 1) * P], xnT[:, j * BANK:(j + 1) * BANK],
                                             start=True, stop=True)
                        m.then_inc(up_done, 1)
                    for n in range(NT):
                        if n % TPB == 0:
                            j = n // TPB
                            pe.wait_ge(h_ready, (t * 2 + e) * nu + FC0 * (j + 1))
                            pe.wait_ge(added, (t * 2 + e) * NT + 1)
                        for f in range(FC0):
                            m = nc.tensor.matmul(bank[4 + n // TPB][:, (n % TPB) * P:(n % TPB + 1) * P],
                                                 hT[:, e, f, n * P:(n + 1) * P], w2s[:, e, f, :],
                                                 start=(f == 0), stop=(f == FC0 - 1))
                        if n % TPB == TPB - 1:
                            m.then_inc(down_done, 1)

            transposes(2)
            pe.wait_ge(added, E * NT + 1)
            for u in range(16):
                b, what, j = u // 8, (u % 8) // 2, u % 2
                if u >= 8:
                    pe.wait_ge(rope_in, u - 7)
                nc.tensor.matmul(bank[u % 8], wl1s[:, what, :], xnT[:, b * S + j * BANK:b * S + (j + 1) * BANK],
                                 start=True, stop=True).then_inc(A[1]["proj"], 1)
            for u in range(4):
                pe.wait_ge(rope_in, 8 + u + 1)
                for t in range(TPB):
                    m = nc.tensor.matmul(bank[u % 8][:, t * P:(t + 1) * P], xnT[:, (u * TPB + t) * P:(u * TPB + t + 1) * P],
                                         wl1s[:, 4, :], start=True, stop=True)
                m.then_inc(A[1]["proj"], 1)
            with pe.Fori(0, G1) as g:
                pe.wait_ge(A[1]["n"], g * L[1].groups + 1)
                pe.wait_ge(kv_ready[0], g * 4 + 4)
                pe.wait_ge(kv_ready[1], g * 5 + 6)
                attention(1, g)
            pe.wait_ge(A[1]["n"], G1 * L[1].groups + 1)
            for n in range(NT):
                for g in range(G1):
                    m = nc.tensor.matmul(bank[n // TPB][:, (n % TPB) * P:(n % TPB + 1) * P],
                                         attn1T[:, n // ST, g, (n % ST) * P:(n % ST + 1) * P], wo1s[:, g, :],
                                         start=(g == 0), stop=(g == G1 - 1))
                if n % TPB == TPB - 1:
                    m.then_inc(y_done[2], 1)

            nc.tensor.matmul(bank[4][0:RANK, 0:D], fbs[:, :], vs[:, :], start=True, stop=True).then_inc(lowA_done, 1)
            pe.wait_ge(lowA_ready, 1)
            nc.tensor.matmul(bank[5], lowA[:, :], uTs[:, :], start=True, stop=True)
            pe.wait_ge(wT_ready, 1)
            for f in range(FC1):
                m = nc.tensor.transpose(bank[6][:, f * P:(f + 1) * P], wfc[:, f, :], ident)
            m.then_inc(w1e_done, 1)
            for f in range(FC1):
                m = nc.tensor.transpose(bank[7][:, f * P:(f + 1) * P], wpj[:, f * P:(f + 1) * P], ident)
            m.then_inc(w2e_done, 1)
            transposes(3)
            pe.wait_ge(w1e_ready, 1)
            pe.wait_ge(w2e_ready, 1)
            for u in range(FC1 * NB):
                f, j = u % FC1, u // FC1
                if u >= 4:
                    pe.wait_ge(relu_ready, u - 3)
                nc.tensor.matmul(bank[4 + u % 4], w1e[:, f * P:(f + 1) * P], xnT[:, j * BANK:(j + 1) * BANK],
                                 start=True, stop=True).then_inc(fc_done, 1)
            for n in range(NT):
                if n % TPB == 0:
                    pe.wait_ge(sq_ready, FC1 * (n // TPB + 1))
                for f in range(FC1):
                    m = nc.tensor.matmul(bank[n // TPB][:, (n % TPB) * P:(n % TPB + 1) * P],
                                         relu[:, f, n * P:(n + 1) * P], w2e[:, f, :],
                                         start=(f == 0), stop=(f == FC1 - 1))
                if n % TPB == TPB - 1:
                    m.then_inc(y_done[3], 1)


def kernel(L0_attn_x, L0_attn_wq, L0_attn_wk, L0_attn_wv, L0_attn_wo, L0_ffn_router_w, L0_ffn_router_b, L0_ffn_w1,
           L0_ffn_b1, L0_ffn_w2, L0_ffn_b2, L1_attn_qkv, L1_attn_wo, L1_ffn_fast_b, L1_ffn_w_fc, L1_ffn_w_proj,
           L1_ffn_u, L1_ffn_v, L1_ffn_gate):
    import concourse.bacc as bacc
    from concourse.bass_utils import run_bass_kernel_spmd

    f = lambda a: np.ascontiguousarray(a)
    w0 = np.stack([np.asarray(w).reshape(CH0, P, D).transpose(0, 2, 1) for w in (L0_attn_wq, L0_attn_wk, L0_attn_wv)], 2)
    qkv = np.asarray(L1_attn_qkv).reshape(3, HEADS, DH1, D)
    swap = (np.arange(DH1) + DH1 // 2) % DH1
    wl1 = np.stack([qkv[0], qkv[0][:, swap], qkv[1], qkv[1][:, swap], qkv[2]]).reshape(5, D, D).transpose(2, 0, 1)
    wo1 = np.zeros((HPG, P // HPG, G1, D), np.asarray(L1_attn_wo).dtype)
    wo1[:, 0:DH1] = np.asarray(L1_attn_wo).T.reshape(G1, HPG, DH1, D).transpose(1, 2, 0, 3)
    arrays = {
        "x": f(np.asarray(L0_attn_x).reshape(T, D)), "w0": f(w0), "wo0": f(np.asarray(L0_attn_wo).T),
        "router_w": f(L0_ffn_router_w), "router_b": f(np.asarray(L0_ffn_router_b).reshape(1, E)),
        "w1": f(L0_ffn_w1), "b1": f(np.asarray(L0_ffn_b1).reshape(E, FC0, P).transpose(2, 0, 1)),
        "w2": f(L0_ffn_w2), "b2": f(L0_ffn_b2),
        "wl1": f(wl1), "wo1": f(wo1.reshape(P, G1, D)), "fast_bT": f(np.asarray(L1_ffn_fast_b).T),
        "w_fc": f(L1_ffn_w_fc), "w_proj": f(L1_ffn_w_proj), "uT": f(np.asarray(L1_ffn_u).T), "v": f(L1_ffn_v),
        "gate": f(np.asarray(L1_ffn_gate).reshape(1, 1)), "consts": constant_table(), "rotary": rotary_table(),
    }
    nc = bacc.Bacc("TRN2", target_bir_lowering=False, num_devices=1)
    args = [nc.dram_tensor(f"in_{n}", a.shape, mybir.dt.from_np(a.dtype), kind="ExternalInput").ap() for n, a in arrays.items()]
    out = nc.dram_tensor("out", (T, D), F32, kind="ExternalOutput").ap()
    build(nc, *args, out)
    r = run_bass_kernel_spmd(nc, [{f"in_{n}": a for n, a in arrays.items()}], core_ids=[0])
    return r.results[0]["out"].reshape(B, S, D)
```

```python
from contextlib import ExitStack

import numpy as np

import concourse.bass as bass
from concourse import mybir

F32 = mybir.dt.float32
BF16 = mybir.dt.bfloat16
U32 = mybir.dt.uint32
ALU = mybir.AluOpType
ACT = mybir.ActivationFunctionType
AX = mybir.AxisListType

P = 128
B, S, D = 2, 1024, 128
T = B * S
NT = T // P
ST = S // P
BANK = 512
TPB = BANK // P
NB = T // BANK
HEADS = 16
DH0 = 64
HPC = P // DH0
CH0 = HEADS // HPC
DH1 = D // HEADS
HPG = 4
G1 = HEADS // HPG
E, TOPK, F0 = 8, 2, 256
CAP = -(-T * TOPK * 5 // (E * 4))
FC0 = F0 // P
F1 = 512
FC1 = F1 // P
RANK = 16
NPROB = 3
TBANKS = 3
QUEUED = 4
NMASK = 4
EPS = 1e-5
MASKED = -1e30

F32R = mybir.dt.float32r
PARTS = 3
STACK = PARTS * PARTS * DH1
KIB = 1024
REGION = 148

C_IDENT, C_CAUSAL, C_UPPER, C_IOTA, C_END = 0, 128, 256, 384, 392


def constant_table():
    c = np.zeros((P, C_END), np.float32)
    i = np.arange(P)
    c[:, C_IDENT:C_IDENT + P] = np.eye(P)
    c[:, C_CAUSAL:C_CAUSAL + P] = np.where(i[None, :] > i[:, None], MASKED, 0.0)
    c[:, C_UPPER:C_UPPER + P] = i[:, None] < i[None, :]
    c[:, C_IOTA:C_IOTA + E] = np.arange(E)
    return c


def rotary_table():
    inv = (1.0 / np.float32(10000.0) ** (np.arange(0, DH1, 2, dtype=np.float32) / np.float32(DH1))).astype(np.float32)
    angle = np.arange(S, dtype=np.float32)[None, :] * inv[:, None]
    cos, sin = np.cos(angle), np.sin(angle)
    cos8, sin8 = np.concatenate([cos, cos]), np.concatenate([-sin, sin])
    return np.ascontiguousarray(np.stack([np.tile(cos8, (HEADS, 1)), np.tile(sin8, (HEADS, 1))], 1), np.float32)


class Attention:

    def __init__(self, heads, copies, project):
        self.heads = heads
        self.order = [(0, qt) for qt in range(ST)] + [(1, qt) for qt in reversed(range(ST))]
        self.items = [(b, qt, h) for b, qt in self.order for h in range(heads)]
        self.n = len(self.items)
        self.groups = B * ST
        self.rounds = []
        self.at_step = [[] for _ in range(self.n + 8)]
        self.copied = {"act": 0, "dve": 0}
        self.round_of = {}
        half = self.n // B
        for step in range(self.n + 2):
            if step >= 2:
                b, qt, h = self.items[step - 2]
                for k0 in range(0, qt + 1, TPB):
                    self.add(step, "T", (step - 2, k0, min(TPB, qt + 1 - k0)), [copies[len(self.rounds) % len(copies)]])
                self.round_of[step - 2] = len(self.rounds) - 1
            if project:
                for other, first in ((1, 2), (0, half + 4)):
                    u, odd = divmod(step - first, 2)
                    if 0 <= u < 6 and not odd:
                        self.project(step, other, u)
        self.n_rounds = len(self.rounds)

    def project(self, step, b, u):
        self.add(step, "P", (b, u // 2, u % 2), ["act"] if u // 2 == 2 else ["act", "dve"])

    def add(self, step, what, args, engines):
        for e in engines:
            self.copied[e] += 1
        self.at_step[step].append(len(self.rounds))
        self.rounds.append((what, args, {e: self.copied[e] for e in engines}))

    def group(self, i):
        return i // self.heads

    def ends_group(self, i):
        return 0 <= i < self.n and self.items[i][2] == self.heads - 1

    def copies_until(self, step):
        last = {}
        for r in range(len(self.rounds)):
            if any(r in self.at_step[x] for x in range(step + 1)):
                last.update(self.rounds[r][2])
        return last


def stage_order(k):
    y = {"y moments": 0, "y norm": 1} if k == 2 else {"y moments": 0, "y norm": 0}
    x = {"x moments": 2, "x norm": 3} if k == 2 else {"x norm": 1, "x moments": 0}
    if k == 0 or k == 4:
        steps = x if k == 0 else {"y moments": 0, "y norm": 1}
    else:
        steps = {**y, **x} if k == 2 else {"y moments": 0, "x norm": 1, "y norm": 0, "x moments": 0}
    return [(what, step - lag) for step in range(NB + 3) for what, lag in steps.items() if 0 <= step - lag < NB]


def build(nc, x, w0, wo0, router_w, router_b, w1, b1, w2, b2, wl1, wo1, fast_bT, w_fc, w_proj, uT, v, gate,
          consts, rotary, out):
    with ExitStack() as ctx:
        def sb(name, shape, dt=F32):
            return ctx.enter_context(nc.sbuf_tensor(name, shape, dt))

        def sem(name):
            return ctx.enter_context(nc.semaphore(name))

        region_at = -(-nc.sbuf_base // 64) * 64
        sb("region", [P, (REGION * KIB + region_at - nc.sbuf_base) // 4 + 8])

        def at(kib, name, shape, dt=F32):
            return nc.alloc_sbuf_tensor_at(name, shape, dt, offset=region_at + kib * KIB)

        attnT = at(0, "attnT", [P, B, CH0, S])
        QTh = at(64, "QTh", [P, B, S], F32R)
        QTl = at(72, "QTl", [P, B, S], F32R)
        Kzh = at(80, "Kzh", [P, B, HPC, S], F32R)
        Kzl = at(96, "Kzl", [P, B, HPC, S], F32R)
        V0 = at(112, "V0", [P, B, ST, P])
        PT0 = at(120, "PT0", [P, 2, HPC, S])
        probs = at(136, "probs", [P, NPROB, S])
        yn = at(136, "yn", [P, 2, TPB, D])
        hT = at(0, "hT", [P, 2, FC0, T])
        acc = at(32, "acc", [P, NT, D])
        wgT = at(40, "wgT", [E, T])
        router = at(48, "router", [P, 8, NT, E])
        lg, ex, top, before, wgt, sel0, sel1, keep = (router[:, n, :, :] for n in range(8))
        idx = at(52, "idx", [P, NT, 8], U32)
        selb = at(53, "selb", [P, NT, E], BF16)
        beforeb = at(54, "beforeb", [P, NT, E], BF16)
        attn1T = at(0, "attn1T", [P, B, G1, S])
        V1 = at(32, "V1", [P, NT, P])
        Zb = at(40, "Zb", [P, NMASK, S], BF16)
        Sm = at(48, "Sm", [P, NMASK, S])
        cs = at(56, "cs", [P, 2, S])
        QS = at(64, "QS", [P, B, HPG, S], BF16)
        KS = at(80, "KS", [P, B, HPG, S], BF16)
        rot = at(96, "rot", [P, 8, S])
        PT1 = at(96, "PT1", [P, 2, HPG, S])
        Vz = at(128, "Vz", [P, B, ST, P])
        parts = at(136, "parts", [P, 2, PARTS, S], BF16)
        relu = at(0, "relu", [P, FC1, T])

        X = sb("X", [P, NT, D])
        xn = sb("xn", [P, NT, D])
        xnT = sb("xnT", [P, T])
        stats = sb("stats", [P, 2, NT, 6])
        mv = sb("mv", [P, 2, NT, 2])
        rstd = sb("rstd", [P, 2, NT])
        power = sb("power", [P, TPB])
        cst = sb("cst", [P, C_END])
        identb = sb("identb", [P, P], BF16)
        causalb = sb("causalb", [P, P], BF16)
        upperb = sb("upperb", [P, P], BF16)
        onesb = sb("onesb", [P, P], BF16)
        onesf = sb("onesf", [1, P])
        ident = cst[:, C_IDENT:C_IDENT + P]
        den = sb("den", [P, 4, HPG])
        rden = sb("rden", [P, 2, HPG])
        rdb = sb("rdb", [P, 2, P])
        rs = sb("rs", [P, 2, P])
        nmax = sb("nmax", [P, 4])
        scratch = sb("scratch", [1, 1])
        credit = sb("credit", [1, 3])
        m1 = sb("m1", [P, NT])
        idxf = sb("idxf", [P, NT, TOPK])
        gsum = sb("gsum", [P, NT])
        wcol = sb("wcol", [P, 2, NT])

        w0s = sb("w0s", [P, 3, P])
        wo0s = sb("wo0s", [P, CH0, D])
        rws = sb("rws", [P, E])
        rbs = sb("rbs", [1, E])
        w1s = sb("w1s", [P, 2, F0])
        w2s = sb("w2s", [P, 2, FC0, D])
        b1s = sb("b1s", [P, E, FC0])
        b1e = sb("b1e", [P, 2, FC0])
        b2s = sb("b2s", [E, D])
        wl1s = sb("wl1s", [P, 5, P])
        wo1s = sb("wo1s", [P, G1, D])
        fbs = sb("fbs", [RANK, RANK])
        uTs = sb("uTs", [RANK, F1])
        vs = sb("vs", [RANK, D])
        gates = sb("gates", [RANK, 1])
        wfc = sb("wfc", [P, FC1, D])
        wpj = sb("wpj", [P, F1])
        wq_t = sb("wq_t", [P, 2, F1])
        wsc, half_up, half_down = (sb(n, [P, FC1 + 1]) for n in ("wsc", "half_up", "half_down"))
        lowA = sb("lowA", [RANK, D])
        w1e = wq_t[:, 0, :]
        w2e = wq_t[:, 1, :].rearrange("p (c d) -> p c d", c=FC1)

        split = nc.dram_tensor("split", (2, PARTS, D, T), BF16, kind="Internal").ap()

        pS = [ctx.enter_context(nc.psum_tensor(f"pS{i}", [P, 2 * BANK], F32)) for i in range(2)]
        pT = [ctx.enter_context(nc.psum_tensor(f"pT{i}", [P, BANK], F32)) for i in range(TBANKS)]
        pO = ctx.enter_context(nc.psum_tensor("pO", [P, BANK], F32))
        bank = [pS[0][:, 0:BANK], pS[0][:, BANK:2 * BANK], pS[1][:, 0:BANK], pS[1][:, BANK:2 * BANK],
                pT[0][:, :], pT[1][:, :], pT[2][:, :], pO[:, :]]

        ld_x, ld_c = sem("ld_x"), sem("ld_c")
        ld_w0, ld_w = sem("ld_w0"), sem("ld_w")
        ld_rot = sem("ld_rot")
        ld_e = [sem("ld_e0"), sem("ld_e1")]
        const_ready = sem("const_ready")
        zeros_ready = sem("zeros_ready")
        st = [[sem(f"st_{w}{k}") for k in range(5)] for w in "yx"]
        var = [[sem(f"var_{w}{k}") for k in range(5)] for w in "yx"]
        rst = [[sem(f"rstd_{w}{k}") for k in range(5)] for w in "yx"]
        yn_ready = [sem(f"yn_ready{k}") for k in range(5)]
        x_added = [sem(f"x_added{k}") for k in range(5)]
        xn_ready = [sem(f"xn_ready{k}") for k in range(5)]
        tr_done = [sem(f"tr_done{k}") for k in range(5)]
        xnT_ready = [sem(f"xnT_ready{k}") for k in range(5)]
        y_done = [sem(f"y_done{k}") for k in range(5)]
        names = ["s", "mx", "z", "p", "t", "cp_act", "cp_dve", "rd1", "rd", "o", "rs", "n"]
        A = [{n: sem(f"a{k}_{n}") for n in names} for k in range(2)]
        proj1, proj1_copied = sem("proj1"), sem("proj1_copied")
        vz_ready = sem("vz_ready")
        rope, rope_sin, part_a, part_v, part_stored = sem("rope"), sem("rope_sin"), sem("part_a"), sem("part_v"), [sem("part_stored0"), sem("part_stored1")]
        ld_stack = [sem("ld_stack0"), sem("ld_stack1")]
        b1_ready = sem("b1_ready")
        lg_done = sem("lg_done")
        r_ = sem("router_step")
        ex_ready = sem("ex_ready")
        rank_done = sem("rank_done")
        wgt_ready = sem("wgt_ready")
        wgT_done, wgT_ready = sem("wgT_done"), sem("wgT_ready")
        b2_done, acc_ready = sem("b2_done"), sem("acc_ready")
        wcol_ready = sem("wcol_ready")
        up_done, h_ready, down_done, added = sem("up_done"), sem("h_ready"), sem("down_done"), sem("added")
        q_d, q_p = sem("scales_ready"), sem("quant_step")
        lowA_done, lowA_ready = sem("lowA_done"), sem("lowA_ready")
        w1e_done, w2e_done, we_ready = sem("w1e_done"), sem("w2e_done"), sem("we_ready")
        fc_done, relu_ready, sq_pool, sq_dve = sem("fc_done"), sem("relu_ready"), sem("sq_pool"), sem("sq_dve")
        stored = sem("stored")

        L = [Attention(HPC, ["act", "dve"], True), Attention(HPG, ["act"], False)]
        first = Attention(HPC, ["act"], False)
        first.rounds, first.at_step, first.copied = [], [[]], {"act": 0, "dve": 0}
        for u in range(6):
            first.project(0, 0, u)
        AHEAD = [{"t": len(first.rounds), **first.copied}, {"t": 0, "act": 0, "dve": 0}]
        block = ctx.enter_context(nc.Block())

        @block.sync
        def _(sp):
            for j in range(NB):
                sp.dma_start(X[:, j * TPB:(j + 1) * TPB, :],
                             x[j * BANK:(j + 1) * BANK, :].rearrange("(n p) d -> p n d", p=P)).then_inc(ld_x, 16)
            sp.dma_start(cst[:, :], consts).then_inc(ld_c, 16)
            sp.dma_start(w0s[:, :, :], w0[0, :, :, :]).then_inc(ld_w0, 16)
            for dst, src in ((wfc[:, :, :], w_fc.rearrange("(c p) d -> p c d", p=P)), (wpj[:, :], w_proj),
                             (wo0s[:, :, :], wo0.rearrange("(c p) d -> p c d", p=P)),
                             (rws[:, :], router_w), (rbs[:, :], router_b),
                             (b1s[:, :, :], b1), (b2s[:, :], b2),
                             (wl1s[:, :, :], wl1), (wo1s[:, :, :], wo1),
                             (fbs[:, :], fast_bT), (uTs[:, :], uT), (vs[:, :], v),
                             (gates[:, :], gate.to_broadcast([RANK, 1]))):
                sp.dma_start(dst, src).then_inc(ld_w, 16)
            for e in range(2):
                sp.dma_start(w1s[:, e, :], w1[e, :, :]).then_inc(ld_e[e], 16)
                sp.dma_start(w2s[:, e, :, :], w2[e, :, :].rearrange("(c p) d -> p c d", p=P)).then_inc(ld_e[e], 16)
            plan = L[0]
            second = max(r for r, (what, args, _) in enumerate(plan.rounds) if what == "P" and args[0] == 1)
            with sp.Fori(0, CH0 - 1) as c:
                sp.wait_ge(A[0]["t"], c * plan.n_rounds + AHEAD[0]["t"] + second + 1)
                sp.dma_start(w0s[:, :, :], w0[bass.ds(c + 1, 1), :, :, :].rearrange("o p k e -> p (o k) e")).then_inc(ld_w0, 16)
            sp.wait_ge(A[0]["t"], (CH0 - 1) * plan.n_rounds + AHEAD[0]["t"] + second + 1)
            sp.dma_start(w0s[:, :, :], w0[0, :, :, :]).then_inc(ld_w0, 16)
            sp.wait_ge(y_done[1], NB)
            sp.dma_start(cs[:, :, :], rotary).then_inc(ld_rot, 16)
            with sp.Fori(0, E // 2 - 1) as t:
                for e in range(2):
                    sp.wait_ge(down_done, (t * 2 + e) * NB + NB)
                    sp.dma_start(w1s[:, e, :], w1[bass.ds(t * 2 + 2 + e, 1), :, :].rearrange("o p f -> p (o f)")).then_inc(ld_e[e], 16)
                    sp.dma_start(w2s[:, e, :, :], w2[bass.ds(t * 2 + 2 + e, 1), :, :].rearrange("o (c p) d -> p (o c) d", p=P)).then_inc(ld_e[e], 16)
            def stacks(b, g):
                def heads(w, parts):
                    return split[w, parts, bass.ds(g * (HPG * DH1), HPG * DH1), b * S:(b + 1) * S]\
                        .rearrange("k (h d) s -> k d h s", h=HPG)

                for i in range(PARTS):
                    for j in range(PARTS):
                        row = (i * PARTS + j) * DH1
                        sp.dma_start(QS[row:row + DH1, b, :, :], heads(0, slice(i, i + 1)).rearrange("k d h s -> (k d) h s"))\
                            .then_inc(ld_stack[b], 16)
                        sp.dma_start(KS[row:row + DH1, b, :, :], heads(1, slice(j, j + 1)).rearrange("k d h s -> (k d) h s"))\
                            .then_inc(ld_stack[b], 16)

            for i in range(2):
                sp.wait_ge(part_a, 2 * i + 2)
                sp.wait_ge(part_v, 2 * i + 2)
                sp.dma_start(split[i, :, :, 0:S].rearrange("k p s -> p k s"), parts[:, i, :, :]).then_inc(part_stored[i], 16)
            sp.wait_ge(zeros_ready, 5)
            for b in range(B):
                for i in range(2):
                    sp.wait_ge(part_stored[i], 16 * (b + 1))
                stacks(b, 0)
            with sp.Fori(0, G1 - 1) as g:
                for b in range(B):
                    sp.wait_ge(A[1]["s"], g * L[1].n + (b + 1) * L[1].n // B)
                    stacks(b, g + 1)
            for j in range(NB):
                sp.wait_ge(x_added[4], j + 1)
                sp.dma_start(out[j * BANK:(j + 1) * BANK, :].rearrange("(n p) d -> p n d", p=P),
                             X[:, j * TPB:(j + 1) * TPB, :]).then_inc(stored, 16)
            sp.wait_ge(stored, 16 * NB)

        @block.gpsimd
        def _(pool):
            def powers(k):
                for what, j in stage_order(k):
                    if what == "y moments":
                        power_of(k, 0, j)
                    if what == "y norm":
                        t = slice(j * TPB, (j + 1) * TPB)
                        pool.wait_ge(yn_ready[k], j + 1)
                        pool.tensor_tensor(X[:, t, :], X[:, t, :], yn[:, j % 2, :, :], ALU.add).then_inc(x_added[k], 1)
                    if what == "x moments":
                        power_of(k, 1, j)

            def power_of(k, w, j):
                r = rstd[:, w, j * TPB:(j + 1) * TPB]
                pool.wait_ge(var[w][k], j + 1)
                pool.tensor_tensor(r, r, power[:, :], ALU.pow).then_inc(rst[w][k], 1)

            pool.memset(power[:, :], -0.5).then_inc(zeros_ready, 1)
            for j, counted in enumerate((A[0]["n"], A[1]["n"], added)):
                pool.memset(credit[:, j:j + 1], 0.0).then_inc(counted, 1)
            pool.wait_ge(zeros_ready, 1)
            powers(0)
            pool.memset(onesb[:, :], 1.0).then_inc(zeros_ready, 1)
            pool.memset(onesf[:, :], 1.0).then_inc(zeros_ready, 1)

            steps = [0]

            def link(i):
                steps[0] += 1
                i.then_inc(q_p, 1)
                pool.wait_ge(q_p, steps[0])

            def ternary(w, n, t0, t1):
                scale, up, down = wsc[:, n:n + 1], half_up[:, n:n + 1], half_down[:, n:n + 1]
                pool.tensor_scalar(t0, w, up, None, ALU.is_gt)
                link(pool.tensor_scalar(t1, w, down, None, ALU.is_lt))
                link(pool.tensor_tensor(t0, t0, t1, ALU.subtract))
                link(pool.tensor_tensor(t0, t0, w, ALU.subtract))
                link(pool.tensor_tensor(t0, t0, w, ALU.add))
                link(pool.tensor_scalar(w, t0, scale, None, ALU.mult))

            pool.wait_ge(q_d, 4)
            for f in range(FC1):
                ternary(wfc[:, f, :], f, wq_t[:, 0, 0:D], wq_t[:, 1, 0:D])
            ternary(wpj[:, :], FC1, wq_t[:, 0, :], wq_t[:, 1, :])

            powers(1)
            pool.wait_ge(y_done[1], NB)
            pool.memset(acc[:, :, :], 0.0).then_inc(acc_ready, 1)
            pool.wait_ge(acc_ready, 1)
            pool.memset(QS[64:P, :, :, :], 0.0).then_inc(zeros_ready, 1)
            pool.memset(KS[64:P, :, :, :], 0.0).then_inc(zeros_ready, 1)
            pool.wait_ge(zeros_ready, 5)
            powers(2)
            pool.wait_ge(ld_rot, 16)
            for i in range(4):
                pool.wait_ge(proj1_copied, 4 * i + 4)
                pool.tensor_tensor(rot[:, 2 * i + 1, :], rot[:, 2 * i + 1, :], cs[:, 1, :], ALU.mult).then_inc(rope_sin, 1)
            pool.memset(Vz[:, :, :, :], 0.0).then_inc(vz_ready, 1)
            powers(3)
            for u in range(0, FC1 * NB, 2):
                f, j = u % FC1, u // FC1
                r = relu[:, f, j * BANK:(j + 1) * BANK]
                pool.wait_ge(relu_ready, u + 1)
                pool.tensor_tensor(r, r, r, ALU.mult).then_inc(sq_pool, 1)
            powers(4)

        @block.scalar
        def _(act):
            def copies_T(k):
                for j in range(NB):
                    act.wait_ge(tr_done[k], j + 1)
                    nc.scalar.copy(xnT[:, j * BANK:(j + 1) * BANK], bank[4 + j]).then_inc(xnT_ready[k], 1)

            def projected(a, args, p):
                b, what, j = args
                cols = slice(j * BANK, (j + 1) * BANK)
                if what == 0:
                    i = nc.scalar.mul(QTh[:, b, cols], p, DH0 ** -0.5)
                elif what == 1:
                    nc.scalar.copy(Kzh[0:DH0, b, 0, cols], p[0:DH0, :])
                    i = nc.scalar.copy(Kzh[DH0:P, b, 1, cols], p[DH0:P, :])
                else:
                    i = nc.scalar.copy(V0[:, b, j * TPB:(j + 1) * TPB, :], p)
                i.then_inc(a["cp_act"], 1)

            def attention(k, it):
                a, plan, ahead = A[k], L[k], AHEAD[k]
                PT = PT0 if k == 0 else PT1
                for i in range(plan.n + 2):
                    for r in plan.at_step[i]:
                        what, args, copies = plan.rounds[r]
                        if "act" not in copies:
                            continue
                        act.wait_ge(a["t"], it * plan.n_rounds + ahead["t"] + r + 1)
                        if what == "P":
                            projected(a, args, pT[r % TBANKS][:, :])
                            continue
                        item, k0, nk = args
                        h, g = plan.items[item][2], plan.group(item)
                        if g >= 2:
                            act.wait_ge(a["o"], it * plan.groups + g - 1)
                        nc.scalar.copy(PT[:, g % 2, h, k0 * P:(k0 + nk) * P], pT[r % TBANKS][:, 0:nk * P])\
                            .then_inc(a["cp_act"], 1)
                    if i < plan.n:
                        b, qt, h = plan.items[i]
                        n, g = (qt + 1) * P, plan.group(i)
                        if i >= NPROB:
                            act.wait_ge(a["t"], it * plan.n_rounds + ahead["t"] + plan.round_of[i - NPROB] + 1)
                        if g >= 4 and h == 0:
                            act.wait_ge(a["rd1"], it * plan.groups + g - 3)
                        act.wait_ge(a["mx"], it * plan.n + i + 1)
                        src, sign = (pS[i % 2], 1.0) if k == 0 else (Sm[:, i % NMASK, :], -1.0)
                        nc.scalar.activation(probs[:, i % NPROB, 0:n], src[:, 0:n], ACT.Exp,
                                             bias=nmax[:, i % 4:i % 4 + 1], scale=sign,
                                             accum_out=den[:, g % 4, h:h + 1]).then_inc(a["p"], 1)

            copies_T(0)
            for r, (what, args, copies) in enumerate(first.rounds):
                act.wait_ge(A[0]["t"], r + 1)
                projected(A[0], args, pT[r % TBANKS][:, :])
            with act.Fori(0, CH0) as c:
                attention(0, c)

            act.wait_ge(lowA_done, 1)
            nc.scalar.activation(lowA[:, :], bank[4][0:RANK, 0:D], ACT.Copy, scale=gates[:, 0:1]).then_inc(lowA_ready, 1)
            act.wait_ge(w1e_done, 1)
            nc.scalar.copy(w1e[:, :], bank[5]).then_inc(we_ready, 1)
            act.wait_ge(w2e_done, 1)
            nc.scalar.copy(w2e[:, :, :], bank[6]).then_inc(we_ready, 1)

            copies_T(1)
            act.wait_ge(r_, 2)
            nc.scalar.activation(ex[:, :, :], lg[:, :, :], ACT.Exp).then_inc(ex_ready, 1)
            with act.Fori(0, E // 2) as t:
                for e in range(2):
                    act.wait_ge(b1_ready, t * 2 + e + 1)
                    for u in range(FC0 * NB):
                        f, j = u % FC0, u // FC0
                        act.wait_ge(up_done, (t * 2 + e) * (FC0 * NB) + u + 1)
                        nc.scalar.activation(hT[:, e, f, j * BANK:(j + 1) * BANK], bank[u % 4], ACT.Gelu,
                                             bias=b1e[:, e, f:f + 1])\
                            .then_inc(h_ready, 1)
            for j in range(NB):
                act.wait_ge(wgT_done, j + 1)
                nc.scalar.copy(wgT[:, j * BANK:(j + 1) * BANK], bank[j][0:E, :]).then_inc(wgT_ready, 1)

            copies_T(2)
            def part(i, j):
                if j == 0 and i >= 2:
                    act.wait_ge(part_stored[i % 2], 16)
                if j == 0:
                    act.wait_ge(rope, 2 * i + 2)
                else:
                    act.wait_ge(part_v, 2 * i + 1)
                nc.scalar.copy(parts[:, i % 2, j, :], rot[:, 2 * i, :]).then_inc(part_a, 1)

            for u in range(20):
                act.wait_ge(proj1, u + 1)
                if u < 16:
                    nc.scalar.copy(rot[:, u // 2, (u % 2) * BANK:(u % 2 + 1) * BANK], bank[u % 8]).then_inc(proj1_copied, 1)
                else:
                    nc.scalar.copy(V1[:, (u - 16) * TPB:(u - 15) * TPB, :], bank[u % 4]).then_inc(proj1_copied, 1)
                if u in (9, 11, 13, 15):
                    part((u - 9) // 4, (u - 9) // 2 % 2)
            for i in (2, 3):
                part(i, 0)
                part(i, 1)
                act.wait_ge(part_v, 2 * i + 2)
                act.wait_ge(part_a, 2 * i + 2)
                act.dma_start(split[i % 2, :, :, S:2 * S].rearrange("k p s -> p k s"), parts[:, i % 2, :, :])\
                    .then_inc(part_stored[i % 2], 16)
            act.wait_ge(part_stored[0], 32)
            act.wait_ge(part_stored[1], 32)
            with act.Fori(0, G1) as g:
                attention(1, g)

            copies_T(3)
            for u in range(FC1 * NB):
                f, j = u % FC1, u // FC1
                act.wait_ge(fc_done, u + 1)
                nc.scalar.activation(relu[:, f, j * BANK:(j + 1) * BANK], bank[4 + u % 4], ACT.Relu).then_inc(relu_ready, 1)

        @block.vector
        def _(dve):
            def moments(k, w, j, tile):
                for n in range(j * TPB, (j + 1) * TPB):
                    i = nc.vector.bn_stats(stats[:, w, n, :], tile(n))
                i.then_inc(st[w][k], 1)
                dve.wait_ge(st[w][k], 2 * j + 1)
                for n in range(j * TPB, (j + 1) * TPB):
                    i = nc.vector.bn_aggr(mv[:, w, n, :], stats[:, w, n, :])
                i.then_inc(st[w][k], 1)
                dve.wait_ge(st[w][k], 2 * j + 2)
                nc.vector.tensor_scalar_add(rstd[:, w, j * TPB:(j + 1) * TPB], mv[:, w, j * TPB:(j + 1) * TPB, 1], EPS)\
                    .then_inc(var[w][k], 1)

            def norm(k, w, j, tile, to, done):
                dve.wait_ge(rst[w][k], j + 1)
                for n in range(j * TPB, (j + 1) * TPB):
                    i = nc.vector.tensor_scalar(to(n), tile(n), mv[:, w, n, 0:1], rstd[:, w, n:n + 1],
                                                ALU.subtract, ALU.mult)
                i.then_inc(done, 1)

            def norm_stage(k, y, y_ready):
                for what, j in stage_order(k):
                    if what == "y moments":
                        y_ready(j)
                        moments(k, 0, j, y)
                    if what == "y norm":
                        if j >= 2:
                            dve.wait_ge(x_added[k], j - 1)
                        norm(k, 0, j, y, lambda n: yn[:, j % 2, n % TPB, :], yn_ready[k])
                    if what == "x moments":
                        if k > 0:
                            dve.wait_ge(x_added[k], j + 1)
                        else:
                            dve.wait_ge(ld_x, 16 * (j + 1))
                        moments(k, 1, j, lambda n: X[:, n, :])
                    if what == "x norm":
                        norm(k, 1, j, lambda n: X[:, n, :], lambda n: xn[:, n, :], xn_ready[k])

            def y_tile(n):
                return bank[n // TPB][:, (n % TPB) * P:(n % TPB + 1) * P]

            def projected(a, args, p):
                b, what, j = args
                cols = slice(j * BANK, (j + 1) * BANK)
                if what == 0:
                    i = nc.vector.scalar_tensor_tensor(QTl[:, b, cols], p, DH0 ** -0.5, QTh[:, b, cols].bitcast(F32),
                                                       ALU.mult, ALU.subtract)
                else:
                    nc.vector.tensor_tensor(Kzl[0:DH0, b, 0, cols], p[0:DH0, :], Kzh[0:DH0, b, 0, cols].bitcast(F32), ALU.subtract)
                    i = nc.vector.tensor_tensor(Kzl[DH0:P, b, 1, cols], p[DH0:P, :], Kzh[DH0:P, b, 1, cols].bitcast(F32), ALU.subtract)
                i.then_inc(a["cp_dve"], 1)

            def attention(k, it, put):
                a, plan, ahead = A[k], L[k], AHEAD[k]
                PT = PT0 if k == 0 else PT1

                def factors_out(g):
                    dve.wait_ge(a["o"], it * plan.groups + g + 1)
                    nc.vector.tensor_copy(rs[:, g % 2, :], pO[:, P:2 * P]).then_inc(a["rs"], 1)

                def outputs(g):
                    dve.wait_ge(a["rs"], it * plan.groups + g + 1)
                    nc.vector.tensor_tensor(put(*plan.order[g]), pO[:, 0:P], rs[:, g % 2, :], ALU.mult).then_inc(a["n"], 1)

                def reciprocals(g):
                    dve.wait_ge(a["p"], it * plan.n + (g + 1) * plan.heads)
                    nc.vector.reciprocal(rden[:, g % 2, 0:plan.heads], den[:, g % 4, 0:plan.heads]).then_inc(a["rd1"], 1)

                def spread(g):
                    dve.wait_ge(a["rd1"], it * plan.groups + g + 1)
                    if g >= 2:
                        dve.wait_ge(a["o"], it * plan.groups + g - 1)
                    nc.vector.tensor_copy(
                        rdb[:, g % 2, :].rearrange("p (h w) -> p h w", h=plan.heads),
                        rden[:, g % 2, 0:plan.heads].rearrange("p (h o) -> p h o", o=1).to_broadcast([P, plan.heads, P // plan.heads]))\
                        .then_inc(a["rd"], 1)

                def mask(i):
                    n = (plan.items[i][1] + 1) * P
                    dve.wait_ge(a["s"], it * plan.n + i + 1)
                    if i >= NMASK:
                        dve.wait_ge(a["p"], it * plan.n + i - NMASK + 1)
                    nc.vector.tensor_scalar(Zb[:, i % NMASK, 0:n], pS[i % 2][:, 0:n], 0.0, MASKED,
                                            ALU.is_equal, ALU.mult).then_inc(a["z"], 1)

                def maximum(i):
                    n = (plan.items[i][1] + 1) * P
                    if k == 0:
                        dve.wait_ge(a["s"], it * plan.n + i + 1)
                        if i >= 4:
                            dve.wait_ge(a["p"], it * plan.n + i - 3)
                        nc.vector.tensor_reduce(nmax[:, i % 4:i % 4 + 1], pS[i % 2][:, 0:n], AX.X, ALU.max,
                                                negate=True).then_inc(a["mx"], 1)
                    else:
                        dve.wait_ge(a["z"], it * plan.n + i + 1)
                        nc.vector.memset(scratch[:, :], 0.0)
                        nc.vector.tensor_tensor_reduce(Sm[:, i % NMASK, 0:n], pS[i % 2][:, 0:n], Zb[:, i % NMASK, 0:n],
                                                       -(DH1 ** -0.5), 3e38, ALU.add, ALU.min,
                                                       nmax[:, i % 4:i % 4 + 1]).then_inc(a["mx"], 1)

                for i in range(plan.n + QUEUED + 2):
                    finished = plan.ends_group(i - QUEUED - 1)
                    summed = plan.ends_group(i - 2)
                    if finished:
                        factors_out(plan.group(i - QUEUED - 1))
                    if i < plan.n and k == 1:
                        mask(i)
                    if finished:
                        outputs(plan.group(i - QUEUED - 1))
                    if summed:
                        reciprocals(plan.group(i - 2))
                    if i < plan.n:
                        maximum(i)
                    if summed:
                        spread(plan.group(i - 2))
                    for r in plan.at_step[i]:
                        what, args, copies = plan.rounds[r]
                        if "dve" not in copies:
                            continue
                        if what == "P":
                            dve.wait_ge(a["cp_act"], it * plan.copied["act"] + ahead["act"] + copies["act"])
                            projected(a, args, pT[r % TBANKS][:, :])
                            continue
                        item, k0, nk = args
                        hh, gg = plan.items[item][2], plan.group(item)
                        dve.wait_ge(a["t"], it * plan.n_rounds + ahead["t"] + r + 1)
                        if gg >= 2:
                            dve.wait_ge(a["o"], it * plan.groups + gg - 1)
                        nc.vector.tensor_copy(PT[:, gg % 2, hh, k0 * P:(k0 + nk) * P], pT[r % TBANKS][:, 0:nk * P])\
                            .then_inc(a["cp_dve"], 1)

            for kz in (Kzh, Kzl):
                nc.vector.memzero(kz[DH0:P, :, 0, :])
                i = nc.vector.memzero(kz[0:DH0, :, 1, :])
            dve.wait_ge(ld_c, 16)
            nc.vector.tensor_copy(identb[:, :], ident)
            nc.vector.tensor_copy(causalb[:, :], cst[:, C_CAUSAL:C_CAUSAL + P])
            nc.vector.tensor_copy(upperb[:, :], cst[:, C_UPPER:C_UPPER + P]).then_inc(const_ready, 1)

            norm_stage(0, None, None)
            for r, (what, args, copies) in enumerate(first.rounds):
                if "dve" in copies:
                    dve.wait_ge(A[0]["cp_act"], copies["act"])
                    projected(A[0], args, pT[r % TBANKS][:, :])
            dve.wait_ge(ld_w, 16 * 13)
            nc.vector.tensor_reduce(wsc[:, 0:FC1], wfc[:, :, :], AX.X, ALU.add, apply_absolute_value=True)
            nc.vector.tensor_reduce(wsc[:, FC1:FC1 + 1], wpj[:, :], AX.X, ALU.add, apply_absolute_value=True).then_inc(q_d, 1)
            dve.wait_ge(q_d, 1)
            nc.vector.tensor_scalar(wsc[:, 0:FC1], wsc[:, 0:FC1], 1.0 / D, 1e-5, ALU.mult, ALU.max)
            nc.vector.tensor_scalar(wsc[:, FC1:FC1 + 1], wsc[:, FC1:FC1 + 1], 1.0 / F1, 1e-5, ALU.mult, ALU.max).then_inc(q_d, 1)
            dve.wait_ge(q_d, 2)
            nc.vector.tensor_scalar(half_up[:, :], wsc[:, :], 0.5, None, ALU.mult).then_inc(q_d, 1)
            nc.vector.tensor_scalar(half_down[:, :], wsc[:, :], -0.5, None, ALU.mult).then_inc(q_d, 1)
            with dve.Fori(0, CH0) as c:
                attention(0, c, lambda b, qt: attnT[:, b, bass.ds(c, 1), qt * P:(qt + 1) * P].rearrange("p o q -> p (o q)"))

            def y_ready(k):
                return lambda j: dve.wait_ge(y_done[k], j + 1)

            norm_stage(1, y_tile, y_ready(1))

            dve.wait_ge(lg_done, 1)
            logits = bank[4][:, 0:NT * E].rearrange("p (n e) -> p n e", n=NT)
            nc.vector.tensor_reduce(m1[:, :], logits, AX.X, ALU.max).then_inc(r_, 1)
            dve.wait_ge(r_, 1)
            nc.vector.tensor_tensor(lg, logits,
                                    m1[:, :].rearrange("p (n o) -> p n o", o=1).to_broadcast([P, NT, E]),
                                    ALU.subtract).then_inc(r_, 1)
            dve.wait_ge(ex_ready, 1)
            for n in range(NT):
                i = nc.vector.max(top[:, n, :], ex[:, n, :])
            i.then_inc(r_, 1)
            dve.wait_ge(r_, 3)
            for n in range(NT):
                i = nc.vector.max_index(idx[:, n, :], top[:, n, :], ex[:, n, :])
            i.then_inc(r_, 1)
            dve.wait_ge(r_, 4)
            nc.vector.tensor_copy(idxf[:, :, :], idx[:, :, 0:TOPK]).then_inc(r_, 1)
            dve.wait_ge(r_, 5)
            experts = cst[:, C_IOTA:C_IOTA + E].rearrange("p (o e) -> p o e", o=1).to_broadcast([P, NT, E])
            for k, s in enumerate((sel0, sel1)):
                i = nc.vector.tensor_tensor(s, experts, idxf[:, :, k:k + 1].to_broadcast([P, NT, E]), ALU.is_equal)
            i.then_inc(r_, 1)
            dve.wait_ge(r_, 6)
            nc.vector.tensor_tensor(sel0, sel0, sel1, ALU.add).then_inc(r_, 1)
            dve.wait_ge(r_, 7)
            nc.vector.tensor_copy(selb[:, :, :], sel0)
            nc.vector.tensor_tensor(wgt, sel0, ex, ALU.mult)
            nc.vector.memset(before[:, 0, :], 0.0).then_inc(r_, 1)
            for n in range(1, NT):
                dve.wait_ge(r_, 7 + n)
                nc.vector.tensor_tensor(before[:, n, :], before[:, n - 1, :], sel0[:, n - 1, :], ALU.add).then_inc(r_, 1)
            dve.wait_ge(r_, 7 + NT)
            nc.vector.tensor_copy(beforeb[:, :, :], before).then_inc(r_, 1)
            nc.vector.tensor_reduce(gsum[:, :], wgt, AX.X, ALU.add).then_inc(r_, 1)
            dve.wait_ge(r_, 9 + NT)
            nc.vector.reciprocal(gsum[:, :], gsum[:, :]).then_inc(r_, 1)
            dve.wait_ge(r_, 10 + NT)
            nc.vector.tensor_tensor(wgt, wgt, gsum[:, :].rearrange("p (n o) -> p n o", o=1).to_broadcast([P, NT, E]),
                                    ALU.mult).then_inc(r_, 1)
            dve.wait_ge(rank_done, 1)
            nc.vector.tensor_scalar(keep, bank[5][:, 0:NT * E].rearrange("p (n e) -> p n e", n=NT),
                                    float(CAP), None, ALU.is_lt).then_inc(r_, 1)
            dve.wait_ge(r_, 12 + NT)
            nc.vector.tensor_tensor(wgt, wgt, keep, ALU.mult).then_inc(wgt_ready, 1)
            dve.wait_ge(wgt_ready, 1)
            dve.wait_ge(acc_ready, 1)
            with dve.Fori(0, E // 2) as t:
                dve.wait_ge(added, t * (2 * NT) + 1)
                nc.vector.memset(scratch[:, :], 0.0)
                for e in range(2):
                    nc.vector.tensor_copy(b1e[:, e, :], b1s[:, bass.ds(t * 2 + e, 1), :].rearrange("p o f -> p (o f)"))\
                        .then_inc(b1_ready, 1)
                    nc.vector.tensor_copy(wcol[:, e, :], wgt[:, :, bass.ds(t * 2 + e, 1)].rearrange("p n o -> p (n o)"))\
                        .then_inc(wcol_ready, 1)
                for e in range(2):
                    dve.wait_ge(wcol_ready, t * 2 + 2)
                    for n in range(NT):
                        if n % TPB == 0:
                            dve.wait_ge(down_done, (t * 2 + e) * NB + n // TPB + 1)
                        dve.wait_ge(added, (t * 2 + e) * NT + n + 1)
                        nc.vector.scalar_tensor_tensor(acc[:, n, :], bank[4 + n // TPB][:, (n % TPB) * P:(n % TPB + 1) * P],
                                                       wcol[:, e, n:n + 1], acc[:, n, :], ALU.mult, ALU.add).then_inc(added, 1)
            for j in range(NB):
                a4 = acc[:, j * TPB:(j + 1) * TPB, :]
                dve.wait_ge(b2_done, j + 1)
                nc.vector.tensor_tensor(a4, a4, bank[4 + j].rearrange("p (n d) -> p n d", n=TPB), ALU.add).then_inc(acc_ready, 1)
            norm_stage(2, lambda n: acc[:, n, :], lambda j: dve.wait_ge(acc_ready, j + 2))

            dve.wait_ge(ld_rot, 16)
            def left(i, j):
                to = rot[:, 2 * i, :] if j == 0 else parts[:, i % 2, 2, :]
                dve.wait_ge(part_a, 2 * i + j + 1)
                nc.vector.tensor_tensor(to, rot[:, 2 * i, :], parts[:, i % 2, j, :], ALU.subtract).then_inc(part_v, 1)

            for i in range(5):
                if i < 4:
                    dve.wait_ge(proj1_copied, 4 * i + 2)
                    nc.vector.tensor_tensor(rot[:, 2 * i, :], rot[:, 2 * i, :], cs[:, 0, :], ALU.mult).then_inc(rope, 1)
                if i >= 1:
                    left(i - 1, 0)
                if i < 4:
                    dve.wait_ge(rope, 2 * i + 1)
                    dve.wait_ge(rope_sin, i + 1)
                    nc.vector.tensor_tensor(rot[:, 2 * i, :], rot[:, 2 * i, :], rot[:, 2 * i + 1, :], ALU.add).then_inc(rope, 1)
                if i >= 1:
                    left(i - 1, 1)
            dve.wait_ge(proj1_copied, 20)
            dve.wait_ge(vz_ready, 1)
            with dve.Fori(0, G1) as g:
                dve.wait_ge(A[1]["n"], g * L[1].groups + 1)
                nc.vector.memset(scratch[:, :], 0.0)
                nc.vector.tensor_copy(
                    Vz[:, :, :, :].rearrange("p b t (h w) -> p (b t) h w", h=HPG)[:, :, :, 0:DH1],
                    V1[:, :, bass.ds(g * (HPG * DH1), HPG * DH1)].rearrange("p t (h w) -> p t h w", h=HPG)).then_inc(vz_ready, 1)
                attention(1, g, lambda b, qt: attn1T[:, b, bass.ds(g, 1), qt * P:(qt + 1) * P].rearrange("p o q -> p (o q)"))
            norm_stage(3, y_tile, y_ready(3))
            for u in range(1, FC1 * NB, 2):
                f, j = u % FC1, u // FC1
                r = relu[:, f, j * BANK:(j + 1) * BANK]
                dve.wait_ge(relu_ready, u + 1)
                nc.vector.tensor_tensor(r, r, r, ALU.mult).then_inc(sq_dve, 1)
            norm_stage(4, y_tile, y_ready(4))

        @block.tensor
        def _(pe):
            def transposes(k):
                for n in range(NT):
                    if n % TPB == 0:
                        pe.wait_ge(xn_ready[k], n // TPB + 1)
                    i = nc.tensor.transpose(bank[4 + n // TPB][:, (n % TPB) * P:(n % TPB + 1) * P], xn[:, n, :], ident)
                    if n % TPB == TPB - 1:
                        i.then_inc(tr_done[k], 1)

            def project(args, p):
                b, what, j = args
                if what < 2:
                    return nc.tensor.matmul(p, w0s[:, what, :], xnT[:, b * S + j * BANK:b * S + (j + 1) * BANK],
                                            start=True, stop=True)
                for t in range(TPB):
                    col = b * S + j * BANK + t * P
                    m = nc.tensor.matmul(p[:, t * P:(t + 1) * P], xnT[:, col:col + P], w0s[:, 2, :],
                                         start=True, stop=True)
                return m

            def values(k, it, g, i):
                a, plan, ahead = A[k], L[k], AHEAD[k]
                w = P // plan.heads
                PT, V = (PT0, V0) if k == 0 else (PT1, Vz)
                b, qt = plan.order[g]
                if g >= 1:
                    pe.wait_ge(a["n"], it * plan.groups + g + 1)
                pe.wait_ge(a["rd"], it * plan.groups + g + 1)
                nc.tensor.matmul(pO[:, P:2 * P], rdb[:, g % 2, :], ident, start=True, stop=True)
                for e2, done in plan.copies_until(i - QUEUED + 2).items():
                    pe.wait_ge(a["cp_" + e2], it * plan.copied[e2] + ahead[e2] + done)
                for kt in range(qt + 1):
                    for h in range(plan.heads):
                        m = nc.tensor.matmul(pO[h * w:(h + 1) * w, 0:P], V[:, b, kt, h * w:(h + 1) * w],
                                             PT[:, g % 2, h, kt * P:(kt + 1) * P], start=(kt == 0), stop=(kt == qt),
                                             skip_group_check=True)
                m.then_inc(a["o"], 1)

            def attention(k, it):
                a, plan, ahead = A[k], L[k], AHEAD[k]
                for i in range(plan.n + QUEUED + 1):
                    if i < plan.n:
                        b, qt, h = plan.items[i]
                        q = slice(qt * P, (qt + 1) * P)
                        if k == 0 and i == plan.n // B:
                            for e2, done in plan.copies_until(i - QUEUED + 2).items():
                                pe.wait_ge(a["cp_" + e2], it * plan.copied[e2] + ahead[e2] + done)
                        if i >= 2:
                            pe.wait_ge(a["p"] if k == 0 else a["mx"], it * plan.n + i - 1)
                        if k == 1 and i % (plan.n // B) == 0:
                            pe.wait_ge(ld_stack[b], (it + 1) * (16 * 2 * PARTS * PARTS))
                        for c0 in range(0, qt + 1, TPB):
                            nk = min(TPB, qt + 1 - c0)
                            last = c0 + nk == qt + 1
                            keys = slice(c0 * P, (c0 + nk) * P)
                            if k == 0:
                                pairs = ((QTh[:, b, q], Kzh[:, b, h, keys]), (QTh[:, b, q], Kzl[:, b, h, keys]),
                                         (QTl[:, b, q], Kzh[:, b, h, keys]))
                            else:
                                pairs = ((QS[:, b, h, q], KS[:, b, h, keys]),)
                            for n, (lhs, rhs) in enumerate(pairs):
                                nc.tensor.matmul(pS[i % 2][:, keys], lhs, rhs, start=(n == 0),
                                                 stop=(n == len(pairs) - 1 and not last))
                        nc.tensor.matmul(pS[i % 2][:, q], identb[:, :], causalb[:, :],
                                         start=False, stop=True).then_inc(a["s"], 1)
                    if plan.ends_group(i - QUEUED):
                        values(k, it, plan.group(i - QUEUED), i)
                    if i < plan.n + 2:
                        if i >= 2:
                            pe.wait_ge(a["p"], it * plan.n + i - 1)
                        for r in plan.at_step[i]:
                            what, args, copies = plan.rounds[r]
                            if r >= TBANKS:
                                for e2, c2 in plan.rounds[r - TBANKS][2].items():
                                    pe.wait_ge(a["cp_" + e2], it * plan.copied[e2] + ahead[e2] + c2)
                            if what == "P":
                                if args == (0, 0, 0):
                                    pe.wait_ge(ld_w0, it * 16 + 32)
                                m = project(args, pT[r % TBANKS][:, :])
                            else:
                                item, k0, nk = args
                                for kt in range(nk):
                                    m = nc.tensor.transpose(pT[r % TBANKS][:, kt * P:(kt + 1) * P],
                                                            probs[:, item % NPROB, (k0 + kt) * P:(k0 + kt + 1) * P], ident)
                            m.then_inc(a["t"], 1)

            pe.wait_ge(const_ready, 1)
            transposes(0)
            pe.wait_ge(xnT_ready[0], NB)
            pe.wait_ge(ld_w0, 16)
            for r, (what, args, copies) in enumerate(first.rounds):
                if r >= TBANKS:
                    for e2, c2 in first.rounds[r - TBANKS][2].items():
                        pe.wait_ge(A[0]["cp_" + e2], c2)
                project(args, pT[r % TBANKS][:, :]).then_inc(A[0]["t"], 1)
            with pe.Fori(0, CH0) as c:
                a = A[0]
                pe.wait_ge(a["n"], c * L[0].groups + 1)
                for e2 in ("act", "dve"):
                    pe.wait_ge(a["cp_" + e2], c * L[0].copied[e2] + AHEAD[0][e2])
                attention(0, c)
            pe.wait_ge(A[0]["n"], CH0 * L[0].groups + 1)
            pe.wait_ge(ld_w, 16 * 13)
            for n in range(NT):
                for c in range(CH0):
                    m = nc.tensor.matmul(bank[n // TPB][:, (n % TPB) * P:(n % TPB + 1) * P],
                                         attnT[:, n // ST, c, (n % ST) * P:(n % ST + 1) * P], wo0s[:, c, :],
                                         start=(c == 0), stop=(c == CH0 - 1))
                if n % TPB == TPB - 1:
                    m.then_inc(y_done[1], 1)

            for e2 in ("act", "dve"):
                pe.wait_ge(A[0]["cp_" + e2], CH0 * L[0].copied[e2] + AHEAD[0][e2])
            nc.tensor.matmul(bank[4][0:RANK, 0:D], fbs[:, :], vs[:, :], start=True, stop=True).then_inc(lowA_done, 1)
            pe.wait_ge(q_p, 5 * (FC1 + 1))
            for f in range(FC1):
                m = nc.tensor.transpose(bank[6][:, f * P:(f + 1) * P], wpj[:, f * P:(f + 1) * P], ident)
            m.then_inc(w2e_done, 1)
            pe.wait_ge(lowA_ready, 1)
            for f in range(FC1):
                nc.tensor.matmul(bank[5][:, f * P:(f + 1) * P], lowA[:, :], uTs[:, f * P:(f + 1) * P], start=True, stop=False)
                m = nc.tensor.matmul(bank[5][:, f * P:(f + 1) * P], wfc[:, f, :], ident, start=False, stop=True)
            m.then_inc(w1e_done, 1)
            pe.wait_ge(we_ready, 2)

            transposes(1)
            pe.wait_ge(zeros_ready, 3)
            pe.wait_ge(xnT_ready[1], NB)
            for n in range(NT):
                nc.tensor.matmul(bank[4][:, n * E:(n + 1) * E], xnT[:, n * P:(n + 1) * P], rws[:, :],
                                 start=(n == 0), stop=False, skip_group_check=True)
            nc.tensor.matmul(bank[4][:, 0:NT * E], onesf[:, :], rbs[:, :].rearrange("o (n e) -> o n e", n=1).to_broadcast([1, NT, E]),
                             start=False, stop=True, skip_group_check=True).then_inc(lg_done, 1)
            pe.wait_ge(r_, 8 + NT)
            nc.tensor.matmul(bank[5][:, 0:NT * E], upperb[:, :], selb[:, :, :], start=True, stop=False)
            nc.tensor.matmul(bank[5][:, 0:NT * E], onesb[:, :], beforeb[:, :, :], start=False, stop=True).then_inc(rank_done, 1)
            with pe.Fori(0, E // 2) as t:
                for e in range(2):
                    pe.wait_ge(ld_e[e], t * 32 + 32)
                    nu = FC0 * NB
                    for u in range(nu):
                        f, j = u % FC0, u // FC0
                        if u >= 4:
                            pe.wait_ge(h_ready, (t * 2 + e) * nu + u - 3)
                        m = nc.tensor.matmul(bank[u % 4], w1s[:, e, f * P:(f + 1) * P], xnT[:, j * BANK:(j + 1) * BANK],
                                             start=True, stop=True)
                        m.then_inc(up_done, 1)
                    pe.wait_ge(wgt_ready, 1)
                    for n in range(NT):
                        if n % TPB == 0:
                            j = n // TPB
                            pe.wait_ge(h_ready, (t * 2 + e) * nu + FC0 * (j + 1))
                            pe.wait_ge(added, (t * 2 + e) * NT + 1)
                        for f in range(FC0):
                            m = nc.tensor.matmul(bank[4 + n // TPB][:, (n % TPB) * P:(n % TPB + 1) * P],
                                                 hT[:, e, f, n * P:(n + 1) * P], w2s[:, e, f, :],
                                                 start=(f == 0), stop=(f == FC0 - 1))
                        if n % TPB == TPB - 1:
                            m.then_inc(down_done, 1)
            for n in range(NT):
                m = nc.tensor.transpose(bank[n // TPB][0:E, (n % TPB) * P:(n % TPB + 1) * P], wgt[:, n, :], ident)
                if n % TPB == TPB - 1:
                    m.then_inc(wgT_done, 1)
            pe.wait_ge(added, E * NT + 1)
            for n in range(NT):
                if n % TPB == 0:
                    pe.wait_ge(wgT_ready, n // TPB + 1)
                m = nc.tensor.matmul(bank[4 + n // TPB][:, (n % TPB) * P:(n % TPB + 1) * P], wgT[:, n * P:(n + 1) * P],
                                     b2s[:, :], start=True, stop=True)
                if n % TPB == TPB - 1:
                    m.then_inc(b2_done, 1)

            pe.wait_ge(acc_ready, NB + 1)
            transposes(2)
            pe.wait_ge(xnT_ready[2], NB)
            for u in range(16):
                b, what, j = u // 8, (u % 8) // 2, u % 2
                if u >= 8:
                    pe.wait_ge(proj1_copied, u - 7)
                nc.tensor.matmul(bank[u % 8], wl1s[:, what, :], xnT[:, b * S + j * BANK:b * S + (j + 1) * BANK],
                                 start=True, stop=True).then_inc(proj1, 1)
            for u in range(4):
                pe.wait_ge(proj1_copied, 8 + u + 1)
                for t in range(TPB):
                    m = nc.tensor.matmul(bank[u % 8][:, t * P:(t + 1) * P], xnT[:, (u * TPB + t) * P:(u * TPB + t + 1) * P],
                                         wl1s[:, 4, :], start=True, stop=True)
                m.then_inc(proj1, 1)
            pe.wait_ge(proj1_copied, 20)
            with pe.Fori(0, G1) as g:
                pe.wait_ge(A[1]["n"], g * L[1].groups + 1)
                pe.wait_ge(vz_ready, g + 2)
                attention(1, g)
            pe.wait_ge(A[1]["n"], G1 * L[1].groups + 1)
            for n in range(NT):
                for g in range(G1):
                    m = nc.tensor.matmul(bank[n // TPB][:, (n % TPB) * P:(n % TPB + 1) * P],
                                         attn1T[:, n // ST, g, (n % ST) * P:(n % ST + 1) * P], wo1s[:, g, :],
                                         start=(g == 0), stop=(g == G1 - 1))
                if n % TPB == TPB - 1:
                    m.then_inc(y_done[3], 1)

            transposes(3)
            pe.wait_ge(xnT_ready[3], NB)
            for u in range(FC1 * NB):
                f, j = u % FC1, u // FC1
                if u >= 4:
                    pe.wait_ge(relu_ready, u - 3)
                nc.tensor.matmul(bank[4 + u % 4], w1e[:, f * P:(f + 1) * P], xnT[:, j * BANK:(j + 1) * BANK],
                                 start=True, stop=True).then_inc(fc_done, 1)
            for n in range(NT):
                if n % TPB == 0:
                    pe.wait_ge(sq_pool, FC1 // 2 * (n // TPB + 1))
                    pe.wait_ge(sq_dve, FC1 // 2 * (n // TPB + 1))
                for f in range(FC1):
                    m = nc.tensor.matmul(bank[n // TPB][:, (n % TPB) * P:(n % TPB + 1) * P],
                                         relu[:, f, n * P:(n + 1) * P], w2e[:, f, :],
                                         start=(f == 0), stop=(f == FC1 - 1))
                if n % TPB == TPB - 1:
                    m.then_inc(y_done[4], 1)


def kernel(L0_attn_x, L0_attn_wq, L0_attn_wk, L0_attn_wv, L0_attn_wo, L0_ffn_router_w, L0_ffn_router_b, L0_ffn_w1,
           L0_ffn_b1, L0_ffn_w2, L0_ffn_b2, L1_attn_qkv, L1_attn_wo, L1_ffn_fast_b, L1_ffn_w_fc, L1_ffn_w_proj,
           L1_ffn_u, L1_ffn_v, L1_ffn_gate):
    import concourse.bacc as bacc
    from concourse.bass_utils import run_bass_kernel_spmd

    f = lambda a: np.ascontiguousarray(a)
    w0 = np.stack([np.asarray(w).reshape(CH0, P, D).transpose(0, 2, 1) for w in (L0_attn_wq, L0_attn_wk, L0_attn_wv)], 2)
    qkv = np.asarray(L1_attn_qkv).reshape(3, HEADS, DH1, D)
    swap = (np.arange(DH1) + DH1 // 2) % DH1
    wl1 = np.stack([qkv[0], qkv[0][:, swap], qkv[1], qkv[1][:, swap], qkv[2]]).reshape(5, D, D).transpose(2, 0, 1)
    wo1 = np.zeros((HPG, P // HPG, G1, D), np.asarray(L1_attn_wo).dtype)
    wo1[:, 0:DH1] = np.asarray(L1_attn_wo).T.reshape(G1, HPG, DH1, D).transpose(1, 2, 0, 3)
    arrays = {
        "x": f(np.asarray(L0_attn_x).reshape(T, D)), "w0": f(w0), "wo0": f(np.asarray(L0_attn_wo).T),
        "router_w": f(L0_ffn_router_w), "router_b": f(np.asarray(L0_ffn_router_b).reshape(1, E)),
        "w1": f(L0_ffn_w1), "b1": f(np.asarray(L0_ffn_b1).reshape(E, FC0, P).transpose(2, 0, 1)),
        "w2": f(L0_ffn_w2), "b2": f(L0_ffn_b2),
        "wl1": f(wl1), "wo1": f(wo1.reshape(P, G1, D)), "fast_bT": f(np.asarray(L1_ffn_fast_b).T),
        "w_fc": f(L1_ffn_w_fc), "w_proj": f(L1_ffn_w_proj), "uT": f(np.asarray(L1_ffn_u).T), "v": f(L1_ffn_v),
        "gate": f(np.asarray(L1_ffn_gate).reshape(1, 1)), "consts": constant_table(), "rotary": rotary_table(),
    }
    nc = bacc.Bacc("TRN2", target_bir_lowering=False, num_devices=1)
    args = [nc.dram_tensor(f"in_{n}", a.shape, mybir.dt.from_np(a.dtype), kind="ExternalInput").ap() for n, a in arrays.items()]
    out = nc.dram_tensor("out", (T, D), F32, kind="ExternalOutput").ap()
    build(nc, *args, out)
    r = run_bass_kernel_spmd(nc, [{f"in_{n}": a for n, a in arrays.items()}], core_ids=[0])
    return r.results[0]["out"].reshape(B, S, D)
```

```python
from contextlib import ExitStack

import numpy as np

import concourse.bass as bass
from concourse import mybir

F32 = mybir.dt.float32
BF16 = mybir.dt.bfloat16
U32 = mybir.dt.uint32
ALU = mybir.AluOpType
ACT = mybir.ActivationFunctionType
AX = mybir.AxisListType

P = 128
B, S, D = 2, 1024, 128
T = B * S
NT = T // P
ST = S // P
BANK = 512
TPB = BANK // P
NB = T // BANK
HEADS = 16
DH0 = 64
HPC = P // DH0
CH0 = HEADS // HPC
DH1 = D // HEADS
HPG = 4
G1 = HEADS // HPG
E, TOPK, F0 = 8, 2, 256
CAP = -(-T * TOPK * 5 // (E * 4))
FC0 = F0 // P
UNITS = FC0 * NB
F1 = 512
FC1 = F1 // P
RANK = 16
NPROB = 3
TBANKS = 3
PROJ1 = (0, 1, 2, 3, 6, 7)
QUEUED = 4
NMASK = 4
EPS = 1e-5
MASKED = -1e30

F32R = mybir.dt.float32r
PARTS = 3
STACK = PARTS * PARTS * DH1
KIB = 1024
REGION = 156

C_IDENT, C_CAUSAL, C_UPPER, C_IOTA, C_END = 0, 128, 256, 384, 392


def constant_table():
    c = np.zeros((P, C_END), np.float32)
    i = np.arange(P)
    c[:, C_IDENT:C_IDENT + P] = np.eye(P)
    c[:, C_CAUSAL:C_CAUSAL + P] = np.where(i[None, :] > i[:, None], MASKED, 0.0)
    c[:, C_UPPER:C_UPPER + P] = i[:, None] < i[None, :]
    c[:, C_IOTA:C_IOTA + E] = np.arange(E)
    return c


def rotary_table():
    inv = (1.0 / np.float32(10000.0) ** (np.arange(0, DH1, 2, dtype=np.float32) / np.float32(DH1))).astype(np.float32)
    angle = np.arange(S, dtype=np.float32)[None, :] * inv[:, None]
    cos, sin = np.cos(angle), np.sin(angle)
    cos8, sin8 = np.concatenate([cos, cos]), np.concatenate([-sin, sin])
    return np.ascontiguousarray(np.stack([np.tile(cos8, (HEADS, 1)), np.tile(sin8, (HEADS, 1))], 1), np.float32)


class Attention:

    def __init__(self, heads, copies, project):
        self.heads = heads
        tiles = list(range(ST)) if heads > 2 else [t + h * (ST // 2) for t in range(ST // 2) for h in range(2)]
        self.order = [(0, qt) for qt in tiles] + [(1, qt) for qt in reversed(tiles)]
        self.items = [(b, qt, h) for b, qt in self.order for h in range(heads)]
        self.n = len(self.items)
        self.groups = B * ST
        self.rounds = []
        self.at_step = [[] for _ in range(self.n + 8)]
        self.copied = {"act": 0, "dve": 0}
        self.round_of = {}
        half = self.n // B
        for step in range(self.n + 2):
            if step >= 2:
                b, qt, h = self.items[step - 2]
                for k0 in range(0, qt + 1, TPB):
                    self.add(step, "T", (step - 2, k0, min(TPB, qt + 1 - k0)), [copies[len(self.rounds) % len(copies)]])
                self.round_of[step - 2] = len(self.rounds) - 1
            if project:
                for other, first in ((1, 2), (0, half + 4)):
                    u, odd = divmod(step - first, 2)
                    if 0 <= u < 6 and not odd:
                        self.project(step, other, u)
        self.n_rounds = len(self.rounds)

    def project(self, step, b, u):
        self.add(step, "P", (b, u // 2, u % 2), ["act"] if u // 2 == 2 else ["act", "dve"])

    def add(self, step, what, args, engines):
        for e in engines:
            self.copied[e] += 1
        self.at_step[step].append(len(self.rounds))
        self.rounds.append((what, args, {e: self.copied[e] for e in engines}))

    def group(self, i):
        return i // self.heads

    def ends_group(self, i):
        return 0 <= i < self.n and self.items[i][2] == self.heads - 1

    def copies_until(self, step):
        last = {}
        for r in range(len(self.rounds)):
            if any(r in self.at_step[x] for x in range(step + 1)):
                last.update(self.rounds[r][2])
        return last


def shift(k, qt):
    n = (qt + 1) * P
    return BANK // 2 if k == 0 and BANK < n < BANK + BANK // 2 else 0


def stage_order(k):
    if k == 0:
        lags = {"x norm": 1, "x moments": 0}
    elif k == 2:
        lags = {"y moments": 0, "y norm": 1, "x moments": 2, "x norm": 3}
    elif k == 4:
        lags = {"y moments": 0, "y norm": 1}
    else:
        lags = {"y moments": 0, "x norm": 1, "y norm": 0, "x moments": 0}
    return [(what, step - lag) for step in range(NB + 3) for what, lag in lags.items() if 0 <= step - lag < NB]


def build(nc, x, w0, wo0, router_w, router_b, w1, b1, w2, b2, wl1, wo1, fast_bT, w_fc, w_proj, uT, v, gate,
          consts, rotary, out):
    with ExitStack() as ctx:
        def sb(name, shape, dt=F32):
            return ctx.enter_context(nc.sbuf_tensor(name, shape, dt))

        def sem(name):
            return ctx.enter_context(nc.semaphore(name))

        region_at = -(-nc.sbuf_base // 64) * 64
        sb("region", [P, (REGION * KIB + region_at - nc.sbuf_base) // 4 + 8])

        def at(kib, name, shape, dt=F32):
            return nc.alloc_sbuf_tensor_at(name, shape, dt, offset=region_at + kib * KIB)

        attnT = at(0, "attnT", [P, B, CH0, S])
        Qs = at(64, "Qs", [P, B, HPC, S], F32R)
        Kh = at(80, "Kh", [P, B, HPC, S], F32R)
        Kl = at(96, "Kl", [P, B, HPC, S], F32R)
        Ql = at(148, "Ql", [P, B, S], F32R)
        V0 = at(112, "V0", [P, B, ST, P])
        PT0 = at(120, "PT0", [P, 2, HPC, S])
        probs = at(136, "probs", [P, NPROB, S])
        yn = at(136, "yn", [P, 2, TPB, D])
        hT = at(0, "hT", [P, 2, FC0, T])
        acc = at(32, "acc", [P, NT, D])
        wgT = at(40, "wgT", [E, T])
        router = at(48, "router", [P, 8, NT, E])
        lg, ex, top, before, wgt, sel0, sel1, keep = (router[:, n, :, :] for n in range(8))
        idx = at(52, "idx", [P, NT, 8], U32)
        selb = at(53, "selb", [P, NT, E], BF16)
        beforeb = at(54, "beforeb", [P, NT, E], BF16)
        attn1T = at(0, "attn1T", [P, B, G1, S])
        V1 = at(32, "V1", [P, NT, P])
        Zb = at(40, "Zb", [P, NMASK, S], BF16)
        Sm = at(48, "Sm", [P, NMASK, S])
        cs = at(56, "cs", [P, 2, S])
        QS = at(64, "QS", [P, B, HPG, S], BF16)
        KS = at(80, "KS", [P, B, HPG, S], BF16)
        rot = at(96, "rot", [P, 8, S])
        PT1 = at(96, "PT1", [P, 2, HPG, S])
        Vz = at(128, "Vz", [P, B, ST, P])
        parts = at(136, "parts", [P, 2, PARTS, S], BF16)
        xn = at(148, "xn", [P, NT, D])
        relu = at(0, "relu", [P, FC1, T])

        X = sb("X", [P, NT, D])
        xnT = sb("xnT", [P, T])
        stats = sb("stats", [P, 2, NT, 6])
        mv = sb("mv", [P, 2, NT, 2])
        rstd = sb("rstd", [P, 2, NT])
        power = sb("power", [P, TPB])
        cst = sb("cst", [P, C_END])
        identb = sb("identb", [P, P], BF16)
        causalb = sb("causalb", [P, P], BF16)
        upperb = sb("upperb", [P, P], BF16)
        onesb = sb("onesb", [P, P], BF16)
        onesf = sb("onesf", [1, P])
        ident = cst[:, C_IDENT:C_IDENT + P]
        den = sb("den", [P, 4, HPG])
        rden = sb("rden", [P, 2, HPG])
        rdb = sb("rdb", [P, 2, P])
        rs = sb("rs", [P, 2, P])
        nmax = sb("nmax", [P, 4])
        scratch = sb("scratch", [1, 3])
        credit = sb("credit", [1, 2])
        m1 = sb("m1", [P, NT])
        idxf = sb("idxf", [P, NT, TOPK])
        gsum = sb("gsum", [P, NT])
        wcol = sb("wcol", [P, 2, NT])

        w0s = sb("w0s", [P, 3, P])
        wo0s = sb("wo0s", [P, CH0, D])
        rws = sb("rws", [P, E])
        rbs = sb("rbs", [1, E])
        w1s = sb("w1s", [P, 2, F0])
        w2s = sb("w2s", [P, 2, FC0, D])
        b1s = sb("b1s", [P, E, FC0])
        b1e = sb("b1e", [P, 2, FC0])
        b2s = sb("b2s", [E, D])
        wl1s = sb("wl1s", [P, 5, P])
        wo1s = sb("wo1s", [P, G1, D])
        fbs = sb("fbs", [RANK, RANK])
        uTs = sb("uTs", [RANK, F1])
        vs = sb("vs", [RANK, D])
        gates = sb("gates", [RANK, 1])
        wfc = sb("wfc", [P, FC1, D])
        wpj = sb("wpj", [P, F1])
        wq_t = sb("wq_t", [P, 2, F1])
        wsc, half_up, half_down = (sb(n, [P, FC1 + 1]) for n in ("wsc", "half_up", "half_down"))
        lowA = sb("lowA", [RANK, D])
        w1e = wq_t[:, 0, :]
        w2e = wq_t[:, 1, :].rearrange("p (c d) -> p c d", c=FC1)

        split = nc.dram_tensor("split", (2, PARTS, D, T), BF16, kind="Internal").ap()

        pS = [ctx.enter_context(nc.psum_tensor(f"pS{i}", [P, 2 * BANK], F32)) for i in range(2)]
        pT = [ctx.enter_context(nc.psum_tensor(f"pT{i}", [P, BANK], F32)) for i in range(TBANKS)]
        pO = ctx.enter_context(nc.psum_tensor("pO", [P, BANK], F32))
        bank = [pS[0][:, 0:BANK], pS[0][:, BANK:2 * BANK], pS[1][:, 0:BANK], pS[1][:, BANK:2 * BANK],
                pT[0][:, :], pT[1][:, :], pT[2][:, :], pO[:, :]]

        ld_x, ld_c = sem("ld_x"), sem("ld_c")
        ld_w0, ld_w = sem("ld_w0"), sem("ld_w")
        ld_rot = sem("ld_rot")
        ld_half = [sem("ld_half0"), sem("ld_half1")]
        ld_w1 = [sem("ld_w1_0"), sem("ld_w1_1")]
        ld_w2 = [sem("ld_w2_0"), sem("ld_w2_1")]
        const_ready = sem("const_ready")
        zeros_ready = sem("zeros_ready")
        st = [[sem(f"st_{w}{k}") for k in range(5)] for w in "yx"]
        var = [[sem(f"var_{w}{k}") for k in range(5)] for w in "yx"]
        rst = [[sem(f"rstd_{w}{k}") for k in range(5)] for w in "yx"]
        yn_ready = [sem(f"yn_ready{k}") for k in range(5)]
        x_added = [sem(f"x_added{k}") for k in range(5)]
        xn_ready = [sem(f"xn_ready{k}") for k in range(5)]
        tr_done = [sem(f"tr_done{k}") for k in range(5)]
        xnT_ready = [sem(f"xnT_ready{k}") for k in range(5)]
        y_done = [sem(f"y_done{k}") for k in range(5)]
        names = ["s", "mx", "z", "p", "t", "cp_act", "cp_dve", "rd1", "rd", "o", "rs", "n"]
        A = [{n: sem(f"a{k}_{n}") for n in names} for k in range(2)]
        proj1, proj1_copied = sem("proj1"), sem("proj1_copied")
        vz_ready = sem("vz_ready")
        rope, rope_sin = sem("rope"), sem("rope_sin")
        part_a, part_v = sem("part_a"), sem("part_v")
        part_stored = [sem("part_stored0"), sem("part_stored1")]
        ld_stack = [sem("ld_stack0"), sem("ld_stack1")]
        b1_ready = sem("b1_ready")
        lg_done = sem("lg_done")
        r_ = sem("router_step")
        ex_ready = sem("ex_ready")
        rank_done = sem("rank_done")
        wgt_ready = sem("wgt_ready")
        wgT_done, wgT_ready = sem("wgT_done"), sem("wgT_ready")
        b2_done = sem("b2_done")
        wcol_ready = sem("wcol_ready")
        up_done, h_ready, down_done, added = sem("up_done"), sem("h_ready"), sem("down_done"), sem("added")
        q_d, q_p = sem("scales_ready"), sem("quant_step")
        lowA_done, lowA_ready = sem("lowA_done"), sem("lowA_ready")
        w1e_done, w2e_done, we_ready = sem("w1e_done"), sem("w2e_done"), sem("we_ready")
        fc_done, relu_ready, sq_ready = sem("fc_done"), sem("relu_ready"), sem("sq_ready")
        stored = sem("stored")

        L = [Attention(HPC, ["act", "dve"], True), Attention(HPG, ["act"], False)]
        first = Attention(HPC, ["act"], False)
        first.rounds, first.at_step, first.copied = [], [[]], {"act": 0, "dve": 0}
        for u in range(6):
            first.project(0, 0, u)
        AHEAD = [{"t": len(first.rounds), **first.copied}, {"t": 0, "act": 0, "dve": 0}]
        block = ctx.enter_context(nc.Block())

        @block.sync
        def _(sp):
            for j in range(NB):
                sp.dma_start(X[:, j * TPB:(j + 1) * TPB, :],
                             x[j * BANK:(j + 1) * BANK, :].rearrange("(n p) d -> p n d", p=P)).then_inc(ld_x, 16)
            sp.dma_start(cst[:, :], consts).then_inc(ld_c, 16)
            sp.dma_start(w0s[:, :, :], w0[0, :, :, :]).then_inc(ld_w0, 16)
            for dst, src in ((wfc[:, :, :], w_fc.rearrange("(c p) d -> p c d", p=P)), (wpj[:, :], w_proj),
                             (wo0s[:, :, :], wo0.rearrange("(c p) d -> p c d", p=P)),
                             (rws[:, :], router_w), (rbs[:, :], router_b),
                             (b1s[:, :, :], b1), (b2s[:, :], b2),
                             (wl1s[:, :, :], wl1), (wo1s[:, :, :], wo1),
                             (fbs[:, :], fast_bT), (uTs[:, :], uT), (vs[:, :], v),
                             (gates[:, :], gate.to_broadcast([RANK, 1]))):
                sp.dma_start(dst, src).then_inc(ld_w, 16)
            for e in range(2):
                sp.dma_start(w1s[:, e, :], w1[e, :, :]).then_inc(ld_w1[e], 16)
                sp.dma_start(w2s[:, e, :, :], w2[e, :, :].rearrange("(c p) d -> p c d", p=P)).then_inc(ld_w2[e], 16)
            plan = L[0]
            second = max(r for r, (what, args, _) in enumerate(plan.rounds) if what == "P" and args[0] == 1)

            def halves(rounds, b, it, copied, ahead):
                def counted(what):
                    return next(c["dve"] for w, args, c in rounds if w == "P" and args == (b, what, 1))

                lo, hi = slice(0, DH0), slice(DH0, P)
                sp.wait_ge(A[0]["cp_dve"], it * copied + ahead + counted(0))
                sp.dma_start(Qs[hi, b, 0, :].bitcast(F32), Ql[lo, b, :].bitcast(F32)).then_inc(ld_half[b], 16)
                sp.dma_start(Qs[lo, b, 1, :].bitcast(F32), Ql[hi, b, :].bitcast(F32)).then_inc(ld_half[b], 16)
                sp.wait_ge(A[0]["cp_dve"], it * copied + ahead + counted(1))
                for kx in (Kh, Kl):
                    sp.dma_start(kx[hi, b, 0, :].bitcast(F32), kx[lo, b, 0, :].bitcast(F32)).then_inc(ld_half[b], 16)
                    sp.dma_start(kx[lo, b, 1, :].bitcast(F32), kx[hi, b, 1, :].bitcast(F32)).then_inc(ld_half[b], 16)

            def turn(c, weights):
                halves(plan.rounds, 1, c, plan.copied["dve"], AHEAD[0]["dve"])
                sp.wait_ge(A[0]["t"], c * plan.n_rounds + AHEAD[0]["t"] + second + 1)
                sp.dma_start(w0s[:, :, :], weights).then_inc(ld_w0, 16)
                halves(plan.rounds, 0, c, plan.copied["dve"], AHEAD[0]["dve"])

            halves(first.rounds, 0, 0, 0, 0)
            with sp.Fori(0, CH0 - 1) as c:
                turn(c, w0[bass.ds(c + 1, 1), :, :, :].rearrange("o p k e -> p (o k) e"))
            turn(CH0 - 1, w0[0, :, :, :])
            sp.wait_ge(y_done[1], NB)
            sp.dma_start(cs[:, :, :], rotary).then_inc(ld_rot, 16)
            with sp.Fori(0, E // 2 - 1) as t:
                for e in range(2):
                    sp.wait_ge(up_done, (t * 2 + e) * UNITS + UNITS)
                    sp.dma_start(w1s[:, e, :], w1[bass.ds(t * 2 + 2 + e, 1), :, :].rearrange("o p f -> p (o f)")).then_inc(ld_w1[e], 16)
                    sp.wait_ge(down_done, (t * 2 + e) * NB + NB)
                    sp.dma_start(w2s[:, e, :, :], w2[bass.ds(t * 2 + 2 + e, 1), :, :].rearrange("o (c p) d -> p (o c) d", p=P)).then_inc(ld_w2[e], 16)
            def stacks(b, g):
                def heads(w, parts):
                    return split[w, parts, bass.ds(g * (HPG * DH1), HPG * DH1), b * S:(b + 1) * S]\
                        .rearrange("k (h d) s -> k d h s", h=HPG)

                for i in range(PARTS):
                    for j in range(PARTS):
                        row = (i * PARTS + j) * DH1
                        sp.dma_start(QS[row:row + DH1, b, :, :], heads(0, slice(i, i + 1)).rearrange("k d h s -> (k d) h s"))\
                            .then_inc(ld_stack[b], 16)
                        sp.dma_start(KS[row:row + DH1, b, :, :], heads(1, slice(j, j + 1)).rearrange("k d h s -> (k d) h s"))\
                            .then_inc(ld_stack[b], 16)

            for i in range(2):
                sp.wait_ge(part_a, 2 * i + 2)
                sp.wait_ge(part_v, 2 * i + 2)
                sp.dma_start(split[i, :, :, 0:S].rearrange("k p s -> p k s"), parts[:, i, :, :]).then_inc(part_stored[i], 16)
            sp.wait_ge(zeros_ready, 5)
            for b in range(B):
                for i in range(2):
                    sp.wait_ge(part_stored[i], 16 * (b + 1))
                stacks(b, 0)
            with sp.Fori(0, G1 - 1) as g:
                for b in range(B):
                    sp.wait_ge(A[1]["s"], g * L[1].n + (b + 1) * L[1].n // B)
                    stacks(b, g + 1)
            for j in range(NB):
                sp.wait_ge(x_added[4], j + 1)
                sp.dma_start(out[j * BANK:(j + 1) * BANK, :].rearrange("(n p) d -> p n d", p=P),
                             X[:, j * TPB:(j + 1) * TPB, :]).then_inc(stored, 16)
            sp.wait_ge(stored, 16 * NB)

        @block.gpsimd
        def _(pool):
            def powers(k):
                for what, j in stage_order(k):
                    if what == "y moments":
                        power_of(k, 0, j)
                    if what == "y norm":
                        t = slice(j * TPB, (j + 1) * TPB)
                        pool.wait_ge(yn_ready[k], j + 1)
                        pool.tensor_tensor(X[:, t, :], X[:, t, :], yn[:, j % 2, :, :], ALU.add).then_inc(x_added[k], 1)
                    if what == "x moments":
                        power_of(k, 1, j)

            def power_of(k, w, j):
                r = rstd[:, w, j * TPB:(j + 1) * TPB]
                pool.wait_ge(var[w][k], j + 1)
                pool.tensor_tensor(r, r, power[:, :], ALU.pow).then_inc(rst[w][k], 1)

            pool.memset(power[:, :], -0.5).then_inc(zeros_ready, 1)
            for j, counted in enumerate((A[0]["n"], A[1]["n"])):
                pool.memset(credit[:, j:j + 1], 0.0).then_inc(counted, 1)
            pool.wait_ge(zeros_ready, 1)
            powers(0)
            pool.memset(onesb[:, :], 1.0).then_inc(zeros_ready, 1)
            pool.memset(onesf[:, :], 1.0).then_inc(zeros_ready, 1)

            steps = [0]

            def link(i):
                steps[0] += 1
                i.then_inc(q_p, 1)
                pool.wait_ge(q_p, steps[0])

            def ternary(w, n, t0, t1):
                scale, up, down = wsc[:, n:n + 1], half_up[:, n:n + 1], half_down[:, n:n + 1]
                pool.tensor_scalar(t0, w, up, None, ALU.is_gt)
                link(pool.tensor_scalar(t1, w, down, None, ALU.is_lt))
                link(pool.tensor_tensor(t0, t0, t1, ALU.subtract))
                link(pool.tensor_tensor(t0, t0, w, ALU.subtract))
                link(pool.tensor_tensor(t0, t0, w, ALU.add))
                link(pool.tensor_scalar(w, t0, scale, None, ALU.mult))

            pool.wait_ge(q_d, 4)
            for f in range(FC1):
                ternary(wfc[:, f, :], f, wq_t[:, 0, 0:D], wq_t[:, 1, 0:D])
            ternary(wpj[:, :], FC1, wq_t[:, 0, :], wq_t[:, 1, :])

            powers(1)
            pool.wait_ge(y_done[1], NB)
            pool.wait_ge(rst[1][1], NB)
            pool.wait_ge(ld_half[0], (CH0 + 1) * (16 * 6))
            pool.wait_ge(ld_half[1], CH0 * (16 * 6))
            pool.memset(QS[64:P, :, :, :], 0.0).then_inc(zeros_ready, 1)
            pool.memset(KS[64:P, :, :, :], 0.0).then_inc(zeros_ready, 1)
            pool.wait_ge(zeros_ready, 5)
            powers(2)
            pool.wait_ge(ld_rot, 16)
            for i in range(4):
                pool.wait_ge(proj1_copied, 5 * (i // 2 * 2 + 1) + i % 2 * 2 + 2)
                pool.tensor_tensor(rot[:, 2 * i + 1, :], rot[:, 2 * i + 1, :], cs[:, 1, :], ALU.mult).then_inc(rope_sin, 1)
            pool.memset(Vz[:, :, :, :], 0.0).then_inc(vz_ready, 1)
            powers(3)
            powers(4)

        @block.scalar
        def _(act):
            def copies_T(k):
                for j in range(NB):
                    act.wait_ge(tr_done[k], j + 1)
                    nc.scalar.copy(xnT[:, j * BANK:(j + 1) * BANK], bank[4 + j]).then_inc(xnT_ready[k], 1)

            def projected(a, args, p):
                b, what, j = args
                cols = slice(j * BANK, (j + 1) * BANK)
                if what == 0:
                    nc.scalar.mul(Qs[0:DH0, b, 0, cols], p[0:DH0, :], DH0 ** -0.5)
                    i = nc.scalar.mul(Qs[DH0:P, b, 1, cols], p[DH0:P, :], DH0 ** -0.5)
                elif what == 1:
                    nc.scalar.copy(Kh[0:DH0, b, 0, cols], p[0:DH0, :])
                    i = nc.scalar.copy(Kh[DH0:P, b, 1, cols], p[DH0:P, :])
                else:
                    i = nc.scalar.copy(V0[:, b, j * TPB:(j + 1) * TPB, :], p)
                i.then_inc(a["cp_act"], 1)

            def factors_out(a, plan, it, g):
                act.wait_ge(a["o"], it * plan.groups + g + 1)
                nc.scalar.copy(rs[:, g % 2, :], pO[:, P:2 * P]).then_inc(a["rs"], 1)

            def attention(k, it):
                a, plan, ahead = A[k], L[k], AHEAD[k]
                PT = PT0 if k == 0 else PT1
                for i in range(plan.n + QUEUED + 1):
                    if plan.ends_group(i - QUEUED):
                        factors_out(a, plan, it, plan.group(i - QUEUED))
                    for r in plan.at_step[i]:
                        what, args, copies = plan.rounds[r]
                        if "act" not in copies:
                            continue
                        act.wait_ge(a["t"], it * plan.n_rounds + ahead["t"] + r + 1)
                        if what == "P":
                            projected(a, args, pT[r % TBANKS][:, :])
                            continue
                        item, k0, nk = args
                        h, g = plan.items[item][2], plan.group(item)
                        if g >= 2:
                            act.wait_ge(a["o"], it * plan.groups + g - 1)
                        nc.scalar.copy(PT[:, g % 2, h, k0 * P:(k0 + nk) * P], pT[r % TBANKS][:, 0:nk * P])\
                            .then_inc(a["cp_act"], 1)
                    if i < plan.n:
                        b, qt, h = plan.items[i]
                        n, g = (qt + 1) * P, plan.group(i)
                        if i >= NPROB:
                            act.wait_ge(a["t"], it * plan.n_rounds + ahead["t"] + plan.round_of[i - NPROB] + 1)
                        if g >= 4 and h == 0:
                            act.wait_ge(a["rd1"], it * plan.groups + g - 3)
                        act.wait_ge(a["mx"], it * plan.n + i + 1)
                        src, sign = (pS[i % 2][:, shift(k, qt):], 1.0) if k == 0 else (Sm[:, i % NMASK, :], -1.0)
                        nc.scalar.activation(probs[:, i % NPROB, 0:n], src[:, 0:n], ACT.Exp,
                                             bias=nmax[:, i % 4:i % 4 + 1], scale=sign,
                                             accum_out=den[:, g % 4, h:h + 1]).then_inc(a["p"], 1)

            copies_T(0)
            for r, (what, args, copies) in enumerate(first.rounds):
                act.wait_ge(A[0]["t"], r + 1)
                projected(A[0], args, pT[r % TBANKS][:, :])
            with act.Fori(0, CH0) as c:
                attention(0, c)

            act.wait_ge(lowA_done, 1)
            nc.scalar.activation(lowA[:, :], bank[4][0:RANK, 0:D], ACT.Copy, scale=gates[:, 0:1]).then_inc(lowA_ready, 1)
            act.wait_ge(w1e_done, 1)
            nc.scalar.copy(w1e[:, :], bank[5]).then_inc(we_ready, 1)
            act.wait_ge(w2e_done, 1)
            nc.scalar.copy(w2e[:, :, :], bank[6]).then_inc(we_ready, 1)

            copies_T(1)
            act.wait_ge(r_, 2)
            nc.scalar.activation(ex[:, :, :], lg[:, :, :], ACT.Exp).then_inc(ex_ready, 1)

            def gelus(e, buf):
                act.wait_ge(b1_ready, e + 1)
                for u in range(UNITS):
                    f, j = u % FC0, u // FC0
                    act.wait_ge(up_done, e * UNITS + u + 1)
                    nc.scalar.activation(hT[:, buf, f, j * BANK:(j + 1) * BANK], bank[u % 4], ACT.Gelu,
                                         bias=b1e[:, buf, f:f + 1]).then_inc(h_ready, 1)

            gelus(0, 0)
            for j in range(NB):
                act.wait_ge(wgT_done, j + 1)
                nc.scalar.copy(wgT[:, j * BANK:(j + 1) * BANK], bank[4 + j][0:E, :]).then_inc(wgT_ready, 1)
            with act.Fori(0, E // 2 - 1) as t:
                gelus(t * 2 + 1, 1)
                gelus(t * 2 + 2, 0)
            gelus(E - 1, 1)

            def part(i, j):
                if j == 0 and i >= 2:
                    act.wait_ge(part_stored[i % 2], 16)
                if j == 0:
                    act.wait_ge(rope, 2 * i + 2)
                else:
                    act.wait_ge(part_v, 2 * i + 1)
                nc.scalar.copy(parts[:, i % 2, j, :], rot[:, 2 * i, :]).then_inc(part_a, 1)

            for j in range(-1, NB):
                if j < NB - 1:
                    act.wait_ge(tr_done[2], j + 2)
                    nc.scalar.copy(xnT[:, (j + 1) * BANK:(j + 2) * BANK], bank[4 + (j + 1) % 2]).then_inc(xnT_ready[2], 1)
                if j < 0:
                    continue
                for what in range(5):
                    u = j * 5 + what
                    p = bank[PROJ1[u % len(PROJ1)]]
                    act.wait_ge(proj1, u + 1)
                    if what < 4:
                        to = rot[:, (j // 2) * 4 + what, (j % 2) * BANK:(j % 2 + 1) * BANK]
                    else:
                        to = V1[:, j * TPB:(j + 1) * TPB, :]
                    nc.scalar.copy(to, p).then_inc(proj1_copied, 1)
                    if u in (10, 12, 14, 16):
                        part((u - 10) // 4, (u - 10) // 2 % 2)
            for i in range(2, 4):
                part(i, 0)
                part(i, 1)
                act.wait_ge(part_v, 2 * i + 2)
                act.wait_ge(part_a, 2 * i + 2)
                act.dma_start(split[i % 2, :, :, S:2 * S].rearrange("k p s -> p k s"), parts[:, i % 2, :, :])\
                    .then_inc(part_stored[i % 2], 16)
            act.wait_ge(part_stored[0], 32)
            act.wait_ge(part_stored[1], 32)
            with act.Fori(0, G1) as g:
                attention(1, g)

            for j in range(NB):
                act.wait_ge(tr_done[3], j + 1)
                nc.scalar.copy(xnT[:, j * BANK:(j + 1) * BANK], bank[4 + j % 2]).then_inc(xnT_ready[3], 1)
                for f in range(FC1 + 1):
                    if f < FC1:
                        u = j * FC1 + f
                        act.wait_ge(fc_done, u + 1)
                        nc.scalar.activation(relu[:, f, j * BANK:(j + 1) * BANK], bank[6 + f % 2], ACT.Relu).then_inc(relu_ready, 1)
                    if f >= 1:
                        r = relu[:, f - 1, j * BANK:(j + 1) * BANK]
                        act.wait_ge(relu_ready, j * FC1 + f)
                        nc.scalar.activation(r, r, ACT.Square).then_inc(sq_ready, 1)

        @block.vector
        def _(dve):
            def moments(k, w, j, tile):
                for n in range(j * TPB, (j + 1) * TPB):
                    i = nc.vector.bn_stats(stats[:, w, n, :], tile(n))
                i.then_inc(st[w][k], 1)
                dve.wait_ge(st[w][k], 2 * j + 1)
                for n in range(j * TPB, (j + 1) * TPB):
                    i = nc.vector.bn_aggr(mv[:, w, n, :], stats[:, w, n, :])
                i.then_inc(st[w][k], 1)
                dve.wait_ge(st[w][k], 2 * j + 2)
                nc.vector.tensor_scalar_add(rstd[:, w, j * TPB:(j + 1) * TPB], mv[:, w, j * TPB:(j + 1) * TPB, 1], EPS)\
                    .then_inc(var[w][k], 1)

            def norm(k, w, j, tile, to, done):
                dve.wait_ge(rst[w][k], j + 1)
                for n in range(j * TPB, (j + 1) * TPB):
                    i = nc.vector.tensor_scalar(to(n), tile(n), mv[:, w, n, 0:1], rstd[:, w, n:n + 1],
                                                ALU.subtract, ALU.mult)
                i.then_inc(done, 1)

            def norm_stage(k, y, y_ready):
                for what, j in stage_order(k):
                    if what == "y moments":
                        y_ready(j)
                        moments(k, 0, j, y)
                    if what == "y norm":
                        if j >= 2:
                            dve.wait_ge(x_added[k], j - 1)
                        norm(k, 0, j, y, lambda n: yn[:, j % 2, n % TPB, :], yn_ready[k])
                    if what == "x moments":
                        if k > 0:
                            dve.wait_ge(x_added[k], j + 1)
                        else:
                            dve.wait_ge(ld_x, 16 * (j + 1))
                        moments(k, 1, j, lambda n: X[:, n, :])
                    if what == "x norm":
                        norm(k, 1, j, lambda n: X[:, n, :], lambda n: xn[:, n, :], xn_ready[k])

            def y_tile(n):
                return bank[n // TPB][:, (n % TPB) * P:(n % TPB + 1) * P]

            def projected(a, args, p):
                b, what, j = args
                cols = slice(j * BANK, (j + 1) * BANK)
                if what == 0:
                    nc.vector.scalar_tensor_tensor(Ql[0:DH0, b, cols], p[0:DH0, :], DH0 ** -0.5,
                                                   Qs[0:DH0, b, 0, cols].bitcast(F32), ALU.mult, ALU.subtract)
                    i = nc.vector.scalar_tensor_tensor(Ql[DH0:P, b, cols], p[DH0:P, :], DH0 ** -0.5,
                                                       Qs[DH0:P, b, 1, cols].bitcast(F32), ALU.mult, ALU.subtract)
                else:
                    nc.vector.tensor_tensor(Kl[0:DH0, b, 0, cols], p[0:DH0, :], Kh[0:DH0, b, 0, cols].bitcast(F32), ALU.subtract)
                    i = nc.vector.tensor_tensor(Kl[DH0:P, b, 1, cols], p[DH0:P, :], Kh[DH0:P, b, 1, cols].bitcast(F32), ALU.subtract)
                i.then_inc(a["cp_dve"], 1)

            def attention(k, it, put):
                a, plan, ahead = A[k], L[k], AHEAD[k]
                PT = PT0 if k == 0 else PT1

                def outputs(g):
                    dve.wait_ge(a["rs"], it * plan.groups + g + 1)
                    nc.vector.tensor_tensor(put(*plan.order[g]), pO[:, 0:P], rs[:, g % 2, :], ALU.mult).then_inc(a["n"], 1)

                def reciprocals(g):
                    dve.wait_ge(a["p"], it * plan.n + (g + 1) * plan.heads)
                    nc.vector.reciprocal(rden[:, g % 2, 0:plan.heads], den[:, g % 4, 0:plan.heads]).then_inc(a["rd1"], 1)

                def spread(g):
                    dve.wait_ge(a["rd1"], it * plan.groups + g + 1)
                    if g >= 2:
                        dve.wait_ge(a["o"], it * plan.groups + g - 1)
                    nc.vector.tensor_copy(
                        rdb[:, g % 2, :].rearrange("p (h w) -> p h w", h=plan.heads),
                        rden[:, g % 2, 0:plan.heads].rearrange("p (h o) -> p h o", o=1).to_broadcast([P, plan.heads, P // plan.heads]))\
                        .then_inc(a["rd"], 1)

                def mask(i):
                    n = (plan.items[i][1] + 1) * P
                    dve.wait_ge(a["s"], it * plan.n + i + 1)
                    if i >= NMASK:
                        dve.wait_ge(a["p"], it * plan.n + i - NMASK + 1)
                    nc.vector.tensor_scalar(Zb[:, i % NMASK, 0:n], pS[i % 2][:, 0:n], 0.0, MASKED,
                                            ALU.is_equal, ALU.mult).then_inc(a["z"], 1)

                def maximum(i):
                    qt = plan.items[i][1]
                    n = (qt + 1) * P
                    if k == 0:
                        dve.wait_ge(a["s"], it * plan.n + i + 1)
                        if i >= 4:
                            dve.wait_ge(a["p"], it * plan.n + i - 3)
                        nc.vector.tensor_reduce(nmax[:, i % 4:i % 4 + 1], pS[i % 2][:, shift(k, qt):shift(k, qt) + n], AX.X, ALU.max,
                                                negate=True).then_inc(a["mx"], 1)
                    else:
                        dve.wait_ge(a["z"], it * plan.n + i + 1)
                        nc.vector.memset(scratch[:, 0:1], 0.0)
                        nc.vector.tensor_tensor_reduce(Sm[:, i % NMASK, 0:n], pS[i % 2][:, 0:n], Zb[:, i % NMASK, 0:n],
                                                       -(DH1 ** -0.5), 3e38, ALU.add, ALU.min,
                                                       nmax[:, i % 4:i % 4 + 1]).then_inc(a["mx"], 1)

                for i in range(plan.n + QUEUED + 2):
                    finished = plan.ends_group(i - QUEUED - 1)
                    summed = plan.ends_group(i - 2)
                    if i < plan.n and k == 1:
                        mask(i)
                    if finished:
                        outputs(plan.group(i - QUEUED - 1))
                    if summed:
                        reciprocals(plan.group(i - 2))
                    if i < plan.n:
                        maximum(i)
                    if summed:
                        spread(plan.group(i - 2))
                    for r in plan.at_step[i]:
                        what, args, copies = plan.rounds[r]
                        if "dve" not in copies:
                            continue
                        if what == "P":
                            dve.wait_ge(a["cp_act"], it * plan.copied["act"] + ahead["act"] + copies["act"])
                            projected(a, args, pT[r % TBANKS][:, :])
                            continue
                        item, k0, nk = args
                        hh, gg = plan.items[item][2], plan.group(item)
                        dve.wait_ge(a["t"], it * plan.n_rounds + ahead["t"] + r + 1)
                        if gg >= 2:
                            dve.wait_ge(a["o"], it * plan.groups + gg - 1)
                        nc.vector.tensor_copy(PT[:, gg % 2, hh, k0 * P:(k0 + nk) * P], pT[r % TBANKS][:, 0:nk * P])\
                            .then_inc(a["cp_dve"], 1)

            dve.wait_ge(ld_c, 16)
            nc.vector.tensor_copy(identb[:, :], ident)
            nc.vector.tensor_copy(causalb[:, :], cst[:, C_CAUSAL:C_CAUSAL + P])
            nc.vector.tensor_copy(upperb[:, :], cst[:, C_UPPER:C_UPPER + P]).then_inc(const_ready, 1)

            norm_stage(0, None, None)
            for r, (what, args, copies) in enumerate(first.rounds):
                if "dve" in copies:
                    dve.wait_ge(A[0]["cp_act"], copies["act"])
                    projected(A[0], args, pT[r % TBANKS][:, :])
            dve.wait_ge(ld_w, 16 * 13)
            nc.vector.tensor_reduce(wsc[:, 0:FC1], wfc[:, :, :], AX.X, ALU.add, apply_absolute_value=True)
            nc.vector.tensor_reduce(wsc[:, FC1:FC1 + 1], wpj[:, :], AX.X, ALU.add, apply_absolute_value=True).then_inc(q_d, 1)
            dve.wait_ge(q_d, 1)
            nc.vector.tensor_scalar(wsc[:, 0:FC1], wsc[:, 0:FC1], 1.0 / D, 1e-5, ALU.mult, ALU.max)
            nc.vector.tensor_scalar(wsc[:, FC1:FC1 + 1], wsc[:, FC1:FC1 + 1], 1.0 / F1, 1e-5, ALU.mult, ALU.max).then_inc(q_d, 1)
            dve.wait_ge(q_d, 2)
            nc.vector.tensor_scalar(half_up[:, :], wsc[:, :], 0.5, None, ALU.mult).then_inc(q_d, 1)
            nc.vector.tensor_scalar(half_down[:, :], wsc[:, :], -0.5, None, ALU.mult).then_inc(q_d, 1)
            with dve.Fori(0, CH0) as c:
                attention(0, c, lambda b, qt: attnT[:, b, bass.ds(c, 1), qt * P:(qt + 1) * P].rearrange("p o q -> p (o q)"))

            def y_ready(k):
                return lambda j: dve.wait_ge(y_done[k], j + 1)

            dve.wait_ge(ld_half[0], (CH0 + 1) * (16 * 6))
            dve.wait_ge(ld_half[1], CH0 * (16 * 6))
            norm_stage(1, y_tile, y_ready(1))

            nc.vector.tensor_copy(b1e[:, 0, :], b1s[:, 0, :]).then_inc(b1_ready, 1)
            nc.vector.tensor_copy(b1e[:, 1, :], b1s[:, 1, :]).then_inc(b1_ready, 1)

            dve.wait_ge(lg_done, 1)
            logits = bank[4][:, 0:NT * E].rearrange("p (n e) -> p n e", n=NT)
            nc.vector.tensor_reduce(m1[:, :], logits, AX.X, ALU.max).then_inc(r_, 1)
            dve.wait_ge(r_, 1)
            nc.vector.tensor_tensor(lg, logits,
                                    m1[:, :].rearrange("p (n o) -> p n o", o=1).to_broadcast([P, NT, E]),
                                    ALU.subtract).then_inc(r_, 1)
            dve.wait_ge(ex_ready, 1)
            for n in range(NT):
                i = nc.vector.max(top[:, n, :], ex[:, n, :])
            i.then_inc(r_, 1)
            dve.wait_ge(r_, 3)
            for n in range(NT):
                i = nc.vector.max_index(idx[:, n, :], top[:, n, :], ex[:, n, :])
            i.then_inc(r_, 1)
            dve.wait_ge(r_, 4)
            nc.vector.tensor_copy(idxf[:, :, :], idx[:, :, 0:TOPK]).then_inc(r_, 1)
            dve.wait_ge(r_, 5)
            experts = cst[:, C_IOTA:C_IOTA + E].rearrange("p (o e) -> p o e", o=1).to_broadcast([P, NT, E])
            for k, s in enumerate((sel0, sel1)):
                i = nc.vector.tensor_tensor(s, experts, idxf[:, :, k:k + 1].to_broadcast([P, NT, E]), ALU.is_equal)
            i.then_inc(r_, 1)
            dve.wait_ge(r_, 6)
            nc.vector.tensor_tensor(sel0, sel0, sel1, ALU.add).then_inc(r_, 1)
            dve.wait_ge(r_, 7)
            nc.vector.tensor_copy(selb[:, :, :], sel0)
            nc.vector.tensor_tensor(wgt, sel0, ex, ALU.mult)
            nc.vector.memset(before[:, 0, :], 0.0).then_inc(r_, 1)
            for n in range(1, NT):
                dve.wait_ge(r_, 7 + n)
                nc.vector.tensor_tensor(before[:, n, :], before[:, n - 1, :], sel0[:, n - 1, :], ALU.add).then_inc(r_, 1)
            dve.wait_ge(r_, 7 + NT)
            nc.vector.tensor_copy(beforeb[:, :, :], before).then_inc(r_, 1)
            nc.vector.tensor_reduce(gsum[:, :], wgt, AX.X, ALU.add).then_inc(r_, 1)
            dve.wait_ge(r_, 9 + NT)
            nc.vector.reciprocal(gsum[:, :], gsum[:, :]).then_inc(r_, 1)
            dve.wait_ge(r_, 10 + NT)
            nc.vector.tensor_tensor(wgt, wgt, gsum[:, :].rearrange("p (n o) -> p n o", o=1).to_broadcast([P, NT, E]),
                                    ALU.mult).then_inc(r_, 1)
            dve.wait_ge(rank_done, 1)
            nc.vector.tensor_scalar(keep, bank[5][:, 0:NT * E].rearrange("p (n e) -> p n e", n=NT),
                                    float(CAP), None, ALU.is_lt).then_inc(r_, 1)
            dve.wait_ge(r_, 12 + NT)
            nc.vector.tensor_tensor(wgt, wgt, keep, ALU.mult).then_inc(wgt_ready, 1)
            dve.wait_ge(wgt_ready, 1)
            for j in range(NB):
                dve.wait_ge(b2_done, j + 1)
                nc.vector.tensor_copy(acc[:, j * TPB:(j + 1) * TPB, :], bank[4 + j].rearrange("p (n d) -> p n d", n=TPB))\
                    .then_inc(added, TPB)

            def weighted_sums(t, more):
                dve.wait_ge(added, t * (2 * NT) + NT)
                nc.vector.memset(scratch[:, 0:1], 0.0)
                for e in range(2):
                    nc.vector.tensor_copy(wcol[:, e, :], wgt[:, :, bass.ds(t * 2 + e, 1)].rearrange("p n o -> p (n o)"))\
                        .then_inc(wcol_ready, 1)
                for e in range(2):
                    if more:
                        dve.wait_ge(h_ready, (t * 2 + e) * UNITS + UNITS)
                        nc.vector.memset(scratch[:, 1 + e:2 + e], 0.0)
                        nc.vector.tensor_copy(b1e[:, e, :], b1s[:, bass.ds(t * 2 + 2 + e, 1), :].rearrange("p o f -> p (o f)"))\
                            .then_inc(b1_ready, 1)
                    dve.wait_ge(wcol_ready, t * 2 + 2)
                    for n in range(NT):
                        if n % TPB == 0:
                            dve.wait_ge(down_done, (t * 2 + e) * NB + n // TPB + 1)
                        nc.vector.scalar_tensor_tensor(acc[:, n, :], bank[4 + n // TPB][:, (n % TPB) * P:(n % TPB + 1) * P],
                                                       wcol[:, e, n:n + 1], acc[:, n, :], ALU.mult, ALU.add).then_inc(added, 1)

            with dve.Fori(0, E // 2 - 1) as t:
                weighted_sums(t, True)
            weighted_sums(E // 2 - 1, False)
            norm_stage(2, lambda n: acc[:, n, :], lambda j: dve.wait_ge(added, E * NT + (j + 1) * TPB))

            dve.wait_ge(ld_rot, 16)
            def left(i, j):
                to = rot[:, 2 * i, :] if j == 0 else parts[:, i % 2, 2, :]
                dve.wait_ge(part_a, 2 * i + j + 1)
                nc.vector.tensor_tensor(to, rot[:, 2 * i, :], parts[:, i % 2, j, :], ALU.subtract).then_inc(part_v, 1)

            for i in range(5):
                if i < 4:
                    dve.wait_ge(proj1_copied, 5 * (i // 2 * 2 + 1) + i % 2 * 2 + 1)
                    nc.vector.tensor_tensor(rot[:, 2 * i, :], rot[:, 2 * i, :], cs[:, 0, :], ALU.mult).then_inc(rope, 1)
                if i >= 1:
                    left(i - 1, 0)
                if i < 4:
                    dve.wait_ge(rope, 2 * i + 1)
                    dve.wait_ge(rope_sin, i + 1)
                    nc.vector.tensor_tensor(rot[:, 2 * i, :], rot[:, 2 * i, :], rot[:, 2 * i + 1, :], ALU.add).then_inc(rope, 1)
                if i >= 1:
                    left(i - 1, 1)
            dve.wait_ge(proj1_copied, 20)
            dve.wait_ge(vz_ready, 1)
            with dve.Fori(0, G1) as g:
                dve.wait_ge(A[1]["n"], g * L[1].groups + 1)
                nc.vector.memset(scratch[:, 0:1], 0.0)
                nc.vector.tensor_copy(
                    Vz[:, :, :, :].rearrange("p b t (h w) -> p (b t) h w", h=HPG)[:, :, :, 0:DH1],
                    V1[:, :, bass.ds(g * (HPG * DH1), HPG * DH1)].rearrange("p t (h w) -> p t h w", h=HPG)).then_inc(vz_ready, 1)
                attention(1, g, lambda b, qt: attn1T[:, b, bass.ds(g, 1), qt * P:(qt + 1) * P].rearrange("p o q -> p (o q)"))
            norm_stage(3, y_tile, y_ready(3))
            norm_stage(4, y_tile, y_ready(4))

        @block.tensor
        def _(pe):
            def transposes(k):
                for n in range(NT):
                    if n % TPB == 0:
                        pe.wait_ge(xn_ready[k], n // TPB + 1)
                    i = nc.tensor.transpose(bank[4 + n // TPB][:, (n % TPB) * P:(n % TPB + 1) * P], xn[:, n, :], ident)
                    if n % TPB == TPB - 1:
                        i.then_inc(tr_done[k], 1)

            def project(args, p):
                b, what, j = args
                if what < 2:
                    return nc.tensor.matmul(p, w0s[:, what, :], xnT[:, b * S + j * BANK:b * S + (j + 1) * BANK],
                                            start=True, stop=True)
                for t in range(TPB):
                    col = b * S + j * BANK + t * P
                    m = nc.tensor.matmul(p[:, t * P:(t + 1) * P], xnT[:, col:col + P], w0s[:, 2, :],
                                         start=True, stop=True)
                return m

            def values(k, it, g, i):
                a, plan, ahead = A[k], L[k], AHEAD[k]
                w = P // plan.heads
                PT, V = (PT0, V0) if k == 0 else (PT1, Vz)
                b, qt = plan.order[g]
                if g >= 1:
                    pe.wait_ge(a["n"], it * plan.groups + g + 1)
                pe.wait_ge(a["rd"], it * plan.groups + g + 1)
                nc.tensor.transpose(pO[:, P:2 * P], rdb[:, g % 2, :], ident)
                for e2, done in plan.copies_until(i - QUEUED + 2).items():
                    pe.wait_ge(a["cp_" + e2], it * plan.copied[e2] + ahead[e2] + done)
                for kt in range(qt + 1):
                    for h in range(plan.heads):
                        m = nc.tensor.matmul(pO[h * w:(h + 1) * w, 0:P], V[:, b, kt, h * w:(h + 1) * w],
                                             PT[:, g % 2, h, kt * P:(kt + 1) * P], start=(kt == 0), stop=(kt == qt),
                                             skip_group_check=True)
                m.then_inc(a["o"], 1)

            def attention(k, it):
                a, plan, ahead = A[k], L[k], AHEAD[k]
                for i in range(plan.n + QUEUED + 1):
                    if i < plan.n:
                        b, qt, h = plan.items[i]
                        q = slice(qt * P, (qt + 1) * P)
                        if k == 0 and i == plan.n // B:
                            for e2, done in plan.copies_until(i - QUEUED + 2).items():
                                pe.wait_ge(a["cp_" + e2], it * plan.copied[e2] + ahead[e2] + done)
                        if i >= 2:
                            pe.wait_ge(a["p"] if k == 0 else a["mx"], it * plan.n + i - 1)
                        if k == 0 and i % (plan.n // B) == 0:
                            pe.wait_ge(ld_half[b], (it + 1) * (16 * 6))
                        if k == 1 and i % (plan.n // B) == 0:
                            pe.wait_ge(ld_stack[b], (it + 1) * (16 * 2 * PARTS * PARTS))
                        off = shift(k, qt) // P
                        split_at = TPB - off
                        for c0, c1 in ((0, min(qt + 1, split_at)), (split_at, qt + 1)):
                            if c0 >= c1:
                                continue
                            last = c1 == qt + 1
                            if k == 0:
                                c1 = max(c1, 2)
                                lhs, rhs = Qs[:, b, h, q], (Kh, Kl)
                            else:
                                lhs, rhs = QS[:, b, h, q], (KS,)
                            for n, keys in enumerate(rhs):
                                nc.tensor.matmul(pS[i % 2][:, (off + c0) * P:(off + c1) * P], lhs,
                                                 keys[:, b, h, c0 * P:c1 * P], start=(n == 0),
                                                 stop=(n == len(rhs) - 1 and not last))
                        nc.tensor.matmul(pS[i % 2][:, (off + qt) * P:(off + qt + 1) * P], identb[:, :], causalb[:, :],
                                         start=False, stop=True).then_inc(a["s"], 1)
                    if plan.ends_group(i - QUEUED):
                        values(k, it, plan.group(i - QUEUED), i)
                    if i < plan.n + 2:
                        if i >= 2:
                            pe.wait_ge(a["p"], it * plan.n + i - 1)
                        for r in plan.at_step[i]:
                            what, args, copies = plan.rounds[r]
                            if r >= TBANKS:
                                for e2, c2 in plan.rounds[r - TBANKS][2].items():
                                    pe.wait_ge(a["cp_" + e2], it * plan.copied[e2] + ahead[e2] + c2)
                            if what == "P":
                                if args == (0, 0, 0):
                                    pe.wait_ge(ld_w0, it * 16 + 32)
                                m = project(args, pT[r % TBANKS][:, :])
                            else:
                                item, k0, nk = args
                                for kt in range(nk):
                                    m = nc.tensor.transpose(pT[r % TBANKS][:, kt * P:(kt + 1) * P],
                                                            probs[:, item % NPROB, (k0 + kt) * P:(k0 + kt + 1) * P], ident)
                            m.then_inc(a["t"], 1)

            pe.wait_ge(const_ready, 1)
            transposes(0)
            pe.wait_ge(xnT_ready[0], NB)
            pe.wait_ge(ld_w0, 16)
            for r, (what, args, copies) in enumerate(first.rounds):
                if r >= TBANKS:
                    for e2, c2 in first.rounds[r - TBANKS][2].items():
                        pe.wait_ge(A[0]["cp_" + e2], c2)
                project(args, pT[r % TBANKS][:, :]).then_inc(A[0]["t"], 1)
            with pe.Fori(0, CH0) as c:
                a = A[0]
                pe.wait_ge(a["n"], c * L[0].groups + 1)
                for e2 in ("act", "dve"):
                    pe.wait_ge(a["cp_" + e2], c * L[0].copied[e2] + AHEAD[0][e2])
                attention(0, c)
            pe.wait_ge(A[0]["n"], CH0 * L[0].groups + 1)
            pe.wait_ge(ld_w, 16 * 13)
            for n in range(NT):
                for c in range(CH0):
                    m = nc.tensor.matmul(bank[n // TPB][:, (n % TPB) * P:(n % TPB + 1) * P],
                                         attnT[:, n // ST, c, (n % ST) * P:(n % ST + 1) * P], wo0s[:, c, :],
                                         start=(c == 0), stop=(c == CH0 - 1))
                if n % TPB == TPB - 1:
                    m.then_inc(y_done[1], 1)

            for e2 in ("act", "dve"):
                pe.wait_ge(A[0]["cp_" + e2], CH0 * L[0].copied[e2] + AHEAD[0][e2])
            nc.tensor.matmul(bank[4][0:RANK, 0:D], fbs[:, :], vs[:, :], start=True, stop=True).then_inc(lowA_done, 1)
            pe.wait_ge(q_p, 5 * (FC1 + 1))
            for f in range(FC1):
                m = nc.tensor.transpose(bank[6][:, f * P:(f + 1) * P], wpj[:, f * P:(f + 1) * P], ident)
            m.then_inc(w2e_done, 1)
            pe.wait_ge(lowA_ready, 1)
            for f in range(FC1):
                nc.tensor.matmul(bank[5][:, f * P:(f + 1) * P], lowA[:, :], uTs[:, f * P:(f + 1) * P], start=True, stop=False)
                m = nc.tensor.matmul(bank[5][:, f * P:(f + 1) * P], wfc[:, f, :], ident, start=False, stop=True)
            m.then_inc(w1e_done, 1)
            pe.wait_ge(we_ready, 2)

            transposes(1)
            pe.wait_ge(zeros_ready, 3)
            pe.wait_ge(xnT_ready[1], NB)
            for n in range(NT):
                nc.tensor.matmul(bank[4][:, n * E:(n + 1) * E], xnT[:, n * P:(n + 1) * P], rws[:, :],
                                 start=(n == 0), stop=False, skip_group_check=True)
            nc.tensor.matmul(bank[4][:, 0:NT * E], onesf[:, :], rbs[:, :].rearrange("o (n e) -> o n e", n=1).to_broadcast([1, NT, E]),
                             start=False, stop=True, skip_group_check=True).then_inc(lg_done, 1)

            def up(e, buf, first=False):
                pe.wait_ge(ld_w1[buf], (e - buf) * 8 + 16)
                for u in range(UNITS):
                    f, j = u % FC0, u // FC0
                    if not first or u >= 4:
                        pe.wait_ge(h_ready, e * UNITS + u - 3)
                    nc.tensor.matmul(bank[u % 4], w1s[:, buf, f * P:(f + 1) * P], xnT[:, j * BANK:(j + 1) * BANK],
                                     start=True, stop=True).then_inc(up_done, 1)

            def down(e, buf):
                pe.wait_ge(ld_w2[buf], (e - buf) * 8 + 16)
                for n in range(NT):
                    if n % TPB == 0:
                        j = n // TPB
                        pe.wait_ge(h_ready, e * UNITS + FC0 * (j + 1))
                        pe.wait_ge(added, e * NT + (j + 1) * TPB)
                    for f in range(FC0):
                        m = nc.tensor.matmul(bank[4 + n // TPB][:, (n % TPB) * P:(n % TPB + 1) * P],
                                             hT[:, buf, f, n * P:(n + 1) * P], w2s[:, buf, f, :],
                                             start=(f == 0), stop=(f == FC0 - 1))
                    if n % TPB == TPB - 1:
                        m.then_inc(down_done, 1)

            up(0, 0, first=True)
            pe.wait_ge(r_, 8 + NT)
            nc.tensor.matmul(bank[5][:, 0:NT * E], upperb[:, :], selb[:, :, :], start=True, stop=False)
            nc.tensor.matmul(bank[5][:, 0:NT * E], onesb[:, :], beforeb[:, :, :], start=False, stop=True).then_inc(rank_done, 1)
            pe.wait_ge(wgt_ready, 1)
            for n in range(NT):
                m = nc.tensor.transpose(bank[4 + n // TPB][0:E, (n % TPB) * P:(n % TPB + 1) * P], wgt[:, n, :], ident)
                if n % TPB == TPB - 1:
                    m.then_inc(wgT_done, 1)
            for n in range(NT):
                if n % TPB == 0:
                    pe.wait_ge(wgT_ready, n // TPB + 1)
                m = nc.tensor.matmul(bank[4 + n // TPB][:, (n % TPB) * P:(n % TPB + 1) * P], wgT[:, n * P:(n + 1) * P],
                                     b2s[:, :], start=True, stop=True)
                if n % TPB == TPB - 1:
                    m.then_inc(b2_done, 1)
            with pe.Fori(0, E // 2 - 1) as t:
                for e in range(2):
                    up(t * 2 + e + 1, 1 - e)
                    down(t * 2 + e, e)
            up(E - 1, 1)
            down(E - 2, 0)
            down(E - 1, 1)

            pe.wait_ge(added, (E + 1) * NT)
            for j in range(-1, NB):
                if j < NB - 1:
                    pe.wait_ge(xn_ready[2], j + 2)
                    if j >= 1:
                        pe.wait_ge(xnT_ready[2], j)
                    for t in range(TPB):
                        m = nc.tensor.transpose(bank[4 + (j + 1) % 2][:, t * P:(t + 1) * P], xn[:, (j + 1) * TPB + t, :], ident)
                    m.then_inc(tr_done[2], 1)
                if j < 0:
                    continue
                pe.wait_ge(xnT_ready[2], j + 1)
                for what in range(5):
                    u = j * 5 + what
                    if u >= len(PROJ1):
                        pe.wait_ge(proj1_copied, u - len(PROJ1) + 1)
                    p = bank[PROJ1[u % len(PROJ1)]]
                    if what < 4:
                        m = nc.tensor.matmul(p, wl1s[:, what, :], xnT[:, j * BANK:(j + 1) * BANK], start=True, stop=True)
                    else:
                        for t in range(TPB):
                            m = nc.tensor.matmul(p[:, t * P:(t + 1) * P], xnT[:, (j * TPB + t) * P:(j * TPB + t + 1) * P],
                                                 wl1s[:, 4, :], start=True, stop=True)
                    m.then_inc(proj1, 1)
            pe.wait_ge(proj1_copied, 20)
            with pe.Fori(0, G1) as g:
                pe.wait_ge(A[1]["n"], g * L[1].groups + 1)
                pe.wait_ge(vz_ready, g + 2)
                attention(1, g)
            pe.wait_ge(A[1]["n"], G1 * L[1].groups + 1)
            for n in range(NT):
                for g in range(G1):
                    m = nc.tensor.matmul(bank[n // TPB][:, (n % TPB) * P:(n % TPB + 1) * P],
                                         attn1T[:, n // ST, g, (n % ST) * P:(n % ST + 1) * P], wo1s[:, g, :],
                                         start=(g == 0), stop=(g == G1 - 1))
                if n % TPB == TPB - 1:
                    m.then_inc(y_done[3], 1)

            for j in range(NB + 1):
                if j < NB:
                    pe.wait_ge(xn_ready[3], j + 1)
                    if j >= 2:
                        pe.wait_ge(xnT_ready[3], j - 1)
                    for t in range(TPB):
                        m = nc.tensor.transpose(bank[4 + j % 2][:, t * P:(t + 1) * P], xn[:, j * TPB + t, :], ident)
                    m.then_inc(tr_done[3], 1)
                if j >= 1:
                    pe.wait_ge(sq_ready, j * FC1)
                    for t in range(TPB):
                        n = (j - 1) * TPB + t
                        for f in range(FC1):
                            m = nc.tensor.matmul(bank[j - 1][:, t * P:(t + 1) * P], relu[:, f, n * P:(n + 1) * P], w2e[:, f, :],
                                                 start=(f == 0), stop=(f == FC1 - 1))
                    m.then_inc(y_done[4], 1)
                if j < NB:
                    pe.wait_ge(xnT_ready[3], j + 1)
                    for f in range(FC1):
                        u = j * FC1 + f
                        if u >= 2:
                            pe.wait_ge(relu_ready, u - 1)
                        nc.tensor.matmul(bank[6 + f % 2], w1e[:, f * P:(f + 1) * P], xnT[:, j * BANK:(j + 1) * BANK],
                                         start=True, stop=True).then_inc(fc_done, 1)


def kernel(L0_attn_x, L0_attn_wq, L0_attn_wk, L0_attn_wv, L0_attn_wo, L0_ffn_router_w, L0_ffn_router_b, L0_ffn_w1,
           L0_ffn_b1, L0_ffn_w2, L0_ffn_b2, L1_attn_qkv, L1_attn_wo, L1_ffn_fast_b, L1_ffn_w_fc, L1_ffn_w_proj,
           L1_ffn_u, L1_ffn_v, L1_ffn_gate):
    import concourse.bacc as bacc
    from concourse.bass_utils import run_bass_kernel_spmd

    f = lambda a: np.ascontiguousarray(a)
    w0 = np.stack([np.asarray(w).reshape(CH0, P, D).transpose(0, 2, 1) for w in (L0_attn_wq, L0_attn_wk, L0_attn_wv)], 2)
    qkv = np.asarray(L1_attn_qkv).reshape(3, HEADS, DH1, D)
    swap = (np.arange(DH1) + DH1 // 2) % DH1
    wl1 = np.stack([qkv[0], qkv[0][:, swap], qkv[1], qkv[1][:, swap], qkv[2]]).reshape(5, D, D).transpose(2, 0, 1)
    wo1 = np.zeros((HPG, P // HPG, G1, D), np.asarray(L1_attn_wo).dtype)
    wo1[:, 0:DH1] = np.asarray(L1_attn_wo).T.reshape(G1, HPG, DH1, D).transpose(1, 2, 0, 3)
    arrays = {
        "x": f(np.asarray(L0_attn_x).reshape(T, D)), "w0": f(w0), "wo0": f(np.asarray(L0_attn_wo).T),
        "router_w": f(L0_ffn_router_w), "router_b": f(np.asarray(L0_ffn_router_b).reshape(1, E)),
        "w1": f(L0_ffn_w1), "b1": f(np.asarray(L0_ffn_b1).reshape(E, FC0, P).transpose(2, 0, 1)),
        "w2": f(L0_ffn_w2), "b2": f(L0_ffn_b2),
        "wl1": f(wl1), "wo1": f(wo1.reshape(P, G1, D)), "fast_bT": f(np.asarray(L1_ffn_fast_b).T),
        "w_fc": f(L1_ffn_w_fc), "w_proj": f(L1_ffn_w_proj), "uT": f(np.asarray(L1_ffn_u).T), "v": f(L1_ffn_v),
        "gate": f(np.asarray(L1_ffn_gate).reshape(1, 1)), "consts": constant_table(), "rotary": rotary_table(),
    }
    nc = bacc.Bacc("TRN2", target_bir_lowering=False, num_devices=1)
    args = [nc.dram_tensor(f"in_{n}", a.shape, mybir.dt.from_np(a.dtype), kind="ExternalInput").ap() for n, a in arrays.items()]
    out = nc.dram_tensor("out", (T, D), F32, kind="ExternalOutput").ap()
    build(nc, *args, out)
    r = run_bass_kernel_spmd(nc, [{f"in_{n}": a for n, a in arrays.items()}], core_ids=[0])
    return r.results[0]["out"].reshape(B, S, D)
```
